# Optimizing a Trainium2 kernel written in Bass

```python
import numpy as np
import jax
import jax.numpy as jnp

def _softmax(x, axis=-1):
    return jax.nn.softmax(x, axis=axis)

def _gelu(x):
    return jax.nn.gelu(x, approximate=True)

def _silu(x):
    return jax.nn.silu(x)

def _sigmoid(x):
    return jax.nn.sigmoid(x)

def _layernorm(x, axis=-1, eps=1e-05):
    m = jnp.mean(x, axis=axis, keepdims=True)
    v = jnp.var(x, axis=axis, keepdims=True)
    return (x - m) / jnp.sqrt(v + eps)

def _scatter_add(tgt, idx, src, axis=0):
    return tgt.at[idx].add(src)

def _segment_sum(src, seg, n):
    return jax.ops.segment_sum(src, seg, n)
kernel_name = 'mk_conv_preact_d2_conv_nchw256_r2_f67811'

def setup_inputs(seed: int=0):
    np.random.seed(seed)
    _w = jnp.asarray

    def _rec_inputs():
        import jax
        import jax.numpy as jnp
        _gk = jax.random.key(seed)
        x = -0.000125 + 0.9999 * jax.random.normal(jax.random.fold_in(_gk, 1), (2, 128, 128, 128), jnp.float32)
        return x
    x = _rec_inputs()

    def _L0_conv_setup():
        import jax, jax.numpy as jnp
        import numpy as np
        WS = 16
        NH = 8

        def _relative_position_index(ws):
            coords = np.stack(np.meshgrid(np.arange(ws), np.arange(ws), indexing='ij'))
            cf = coords.reshape(2, -1)
            rel = cf[:, :, None] - cf[:, None, :]
            rel = rel.transpose(1, 2, 0)
            rel += ws - 1
            rel[:, :, 0] *= 2 * ws - 1
            return jnp.asarray(rel.sum(-1))
        key = jax.random.key(seed)
        ks = jax.random.split(key, 6)
        B, C, H, W = (2, 128, 128, 128)
        return {'x': jax.random.normal(ks[0], (B, C, H, W), jnp.float32), 'qkv_w': jax.random.normal(ks[1], (3 * C, C), jnp.float32) * 0.02, 'qkv_b': jax.random.normal(ks[2], (3 * C,), jnp.float32) * 0.02, 'proj_w': jax.random.normal(ks[3], (C, C), jnp.float32) * 0.02, 'proj_b': jax.random.normal(ks[4], (C,), jnp.float32) * 0.02, 'bias_table': jax.random.normal(ks[5], ((2 * WS - 1) ** 2, NH), jnp.float32) * 0.02}
    _L0_conv_all = _L0_conv_setup()
    _L0_conv_in = {k: v for k, v in _L0_conv_all.items() if k in ('qkv_w', 'qkv_b', 'proj_w', 'proj_b', 'bias_table')}
    del _L0_conv_all

    def _L1_conv_setup():
        import jax, jax.numpy as jnp
        import numpy as np
        G = 8
        KS = 3
        K = KS * KS
        DIL = 1
        OFFSET_SCALE = 1.0

        def _dcnv4(x, value_proj_w, value_proj_b, offset_mask_w, offset_mask_b, output_proj_w, output_proj_b):
            N, C, H, W = x.shape
            L = H * W
            Cg = C // G
            xt = x.reshape(N, C, L).transpose(0, 2, 1)
            v = xt @ value_proj_w.T + value_proj_b
            om = xt @ offset_mask_w.T + offset_mask_b
            om = om[..., :G * K * 3].reshape(N, H, W, G, 3 * K)
            off = om[..., :2 * K].reshape(N, H, W, G, K, 2)
            mask = om[..., 2 * K:]
            kidx = jnp.arange(KS, dtype=x.dtype) - (KS - 1) / 2
            ky, kx = jnp.meshgrid(kidx, kidx, indexing='ij')
            ky = ky.ravel()
            kx = kx.ravel()
            px = jnp.arange(W, dtype=x.dtype)[None, None, :, None, None]
            py = jnp.arange(H, dtype=x.dtype)[None, :, None, None, None]
            loc_x = px + DIL * kx + off[..., 0] * OFFSET_SCALE
            loc_y = py + DIL * ky + off[..., 1] * OFFSET_SCALE
            x0 = jnp.floor(loc_x)
            y0 = jnp.floor(loc_y)
            wx = loc_x - x0
            wy = loc_y - y0
            x0i = x0.astype(jnp.int32)
            y0i = y0.astype(jnp.int32)
            v_g = v.reshape(N, L, G, Cg)

            def corner(yi, xi, w):
                valid = ((xi >= 0) & (xi < W) & (yi >= 0) & (yi < H)).astype(x.dtype)
                idx = jnp.clip(yi, 0, H - 1) * W + jnp.clip(xi, 0, W - 1)
                idx = idx.transpose(0, 1, 2, 4, 3).reshape(N, L * K, G)
                g = jnp.take_along_axis(v_g, idx[..., None], axis=1)
                g = g.reshape(N, H, W, K, G, Cg)
                wv = (w * valid).transpose(0, 1, 2, 4, 3)
                return g * wv[..., None]
            sampled = corner(y0i, x0i, (1 - wy) * (1 - wx)) + corner(y0i, x0i + 1, (1 - wy) * wx) + corner(y0i + 1, x0i, wy * (1 - wx)) + corner(y0i + 1, x0i + 1, wy * wx)
            mask_t = mask.transpose(0, 1, 2, 4, 3)
            out = jnp.einsum('nhwkgc,nhwkg->nhwgc', sampled, mask_t)
            out = out.reshape(N, L, C) @ output_proj_w.T + output_proj_b
            return out.transpose(0, 2, 1).reshape(N, C, H, W)
        key = jax.random.key(seed)
        ks = jax.random.split(key, 7)
        N, C, H, W = (2, 128, 48, 48)
        OM = int(np.ceil(G * K * 3 / 8) * 8)
        x = jax.random.normal(ks[0], (N, C, H, W), dtype=jnp.float32)
        value_proj_w = jax.random.normal(ks[1], (C, C), dtype=jnp.float32) * (1.0 / np.sqrt(C))
        value_proj_b = jnp.zeros((C,), dtype=jnp.float32)
        offset_mask_w = jax.random.normal(ks[2], (OM, C), dtype=jnp.float32) * 0.02
        offset_mask_b = jnp.zeros((OM,), dtype=jnp.float32)
        output_proj_w = jax.random.normal(ks[3], (C, C), dtype=jnp.float32) * (1.0 / np.sqrt(C))
        output_proj_b = jnp.zeros((C,), dtype=jnp.float32)
        return {'x': x, 'value_proj_w': value_proj_w, 'value_proj_b': value_proj_b, 'offset_mask_w': offset_mask_w, 'offset_mask_b': offset_mask_b, 'output_proj_w': output_proj_w, 'output_proj_b': output_proj_b}
    _L1_conv_all = _L1_conv_setup()
    _L1_conv_in = {k: v for k, v in _L1_conv_all.items() if k in ('value_proj_w', 'value_proj_b', 'offset_mask_w', 'offset_mask_b', 'output_proj_w', 'output_proj_b')}
    del _L1_conv_all
    return {'x': x, 'L0_conv_qkv_w': _L0_conv_in['qkv_w'], 'L0_conv_qkv_b': _L0_conv_in['qkv_b'], 'L0_conv_proj_w': _L0_conv_in['proj_w'], 'L0_conv_proj_b': _L0_conv_in['proj_b'], 'L0_conv_bias_table': _L0_conv_in['bias_table'], 'L1_conv_value_proj_w': _L1_conv_in['value_proj_w'], 'L1_conv_value_proj_b': _L1_conv_in['value_proj_b'], 'L1_conv_offset_mask_w': _L1_conv_in['offset_mask_w'], 'L1_conv_offset_mask_b': _L1_conv_in['offset_mask_b'], 'L1_conv_output_proj_w': _L1_conv_in['output_proj_w'], 'L1_conv_output_proj_b': _L1_conv_in['output_proj_b']}

def reference(x, L0_conv_qkv_w, L0_conv_qkv_b, L0_conv_proj_w, L0_conv_proj_b, L0_conv_bias_table, L1_conv_value_proj_w, L1_conv_value_proj_b, L1_conv_offset_mask_w, L1_conv_offset_mask_b, L1_conv_output_proj_w, L1_conv_output_proj_b):
    import jax
    import jax.numpy as jnp

    def _L0_conv_ref(x, qkv_w, qkv_b, proj_w, proj_b, bias_table):
        import jax, jax.numpy as jnp
        import numpy as np
        WS = 16
        NH = 8

        def _relative_position_index(ws):
            coords = np.stack(np.meshgrid(np.arange(ws), np.arange(ws), indexing='ij'))
            cf = coords.reshape(2, -1)
            rel = cf[:, :, None] - cf[:, None, :]
            rel = rel.transpose(1, 2, 0)
            rel += ws - 1
            rel[:, :, 0] *= 2 * ws - 1
            return jnp.asarray(rel.sum(-1))
        B, C, H, W = x.shape
        ws, nh = (WS, NH)
        hd = C // nh
        N = ws * ws
        scale = hd ** (-0.5)
        xw = x.reshape(B, C, H // ws, ws, W // ws, ws)
        xw = xw.transpose(0, 2, 4, 3, 5, 1).reshape(-1, N, C)
        qkv = xw @ qkv_w.T + qkv_b
        qkv = qkv.reshape(-1, N, 3, nh, hd).transpose(2, 0, 3, 1, 4)
        q, k, v = (qkv[0], qkv[1], qkv[2])
        attn = jnp.einsum('whnd,whmd->whnm', q, k) * scale
        rpi = _relative_position_index(ws)
        bias = bias_table[rpi.reshape(-1)].reshape(N, N, nh).transpose(2, 0, 1)
        attn = jax.nn.softmax(attn + bias[None], axis=-1)
        out = jnp.einsum('whnm,whmd->whnd', attn, v)
        out = out.transpose(0, 2, 1, 3).reshape(-1, ws, ws, C)
        out = out.reshape(B, H // ws, W // ws, ws, ws, C)
        out = out.transpose(0, 5, 1, 3, 2, 4).reshape(B, H, W, C)
        out = out @ proj_w.T + proj_b
        return out.reshape(B, C, H, W)

    def _L1_conv_ref(x, value_proj_w, value_proj_b, offset_mask_w, offset_mask_b, output_proj_w, output_proj_b):
        import jax, jax.numpy as jnp
        import numpy as np
        G = 8
        KS = 3
        K = KS * KS
        DIL = 1
        OFFSET_SCALE = 1.0

        def _dcnv4(x, value_proj_w, value_proj_b, offset_mask_w, offset_mask_b, output_proj_w, output_proj_b):
            N, C, H, W = x.shape
            L = H * W
            Cg = C // G
            xt = x.reshape(N, C, L).transpose(0, 2, 1)
            v = xt @ value_proj_w.T + value_proj_b
            om = xt @ offset_mask_w.T + offset_mask_b
            om = om[..., :G * K * 3].reshape(N, H, W, G, 3 * K)
            off = om[..., :2 * K].reshape(N, H, W, G, K, 2)
            mask = om[..., 2 * K:]
            kidx = jnp.arange(KS, dtype=x.dtype) - (KS - 1) / 2
            ky, kx = jnp.meshgrid(kidx, kidx, indexing='ij')
            ky = ky.ravel()
            kx = kx.ravel()
            px = jnp.arange(W, dtype=x.dtype)[None, None, :, None, None]
            py = jnp.arange(H, dtype=x.dtype)[None, :, None, None, None]
            loc_x = px + DIL * kx + off[..., 0] * OFFSET_SCALE
            loc_y = py + DIL * ky + off[..., 1] * OFFSET_SCALE
            x0 = jnp.floor(loc_x)
            y0 = jnp.floor(loc_y)
            wx = loc_x - x0
            wy = loc_y - y0
            x0i = x0.astype(jnp.int32)
            y0i = y0.astype(jnp.int32)
            v_g = v.reshape(N, L, G, Cg)

            def corner(yi, xi, w):
                valid = ((xi >= 0) & (xi < W) & (yi >= 0) & (yi < H)).astype(x.dtype)
                idx = jnp.clip(yi, 0, H - 1) * W + jnp.clip(xi, 0, W - 1)
                idx = idx.transpose(0, 1, 2, 4, 3).reshape(N, L * K, G)
                g = jnp.take_along_axis(v_g, idx[..., None], axis=1)
                g = g.reshape(N, H, W, K, G, Cg)
                wv = (w * valid).transpose(0, 1, 2, 4, 3)
                return g * wv[..., None]
            sampled = corner(y0i, x0i, (1 - wy) * (1 - wx)) + corner(y0i, x0i + 1, (1 - wy) * wx) + corner(y0i + 1, x0i, wy * (1 - wx)) + corner(y0i + 1, x0i + 1, wy * wx)
            mask_t = mask.transpose(0, 1, 2, 4, 3)
            out = jnp.einsum('nhwkgc,nhwkg->nhwgc', sampled, mask_t)
            out = out.reshape(N, L, C) @ output_proj_w.T + output_proj_b
            return out.transpose(0, 2, 1).reshape(N, C, H, W)
        return _dcnv4(x, value_proj_w, value_proj_b, offset_mask_w, offset_mask_b, output_proj_w, output_proj_b)

    def _gn(v, G=32, eps=1e-05):
        B_, C_, H_, W_ = v.shape
        g = v.reshape(B_, G, C_ // G, H_, W_)
        m = jnp.mean(g, axis=(2, 3, 4), keepdims=True)
        s = jnp.var(g, axis=(2, 3, 4), keepdims=True)
        return ((g - m) / jnp.sqrt(s + eps)).reshape(v.shape)

    def _ln_c(v, eps=1e-06):
        m = jnp.mean(v, axis=1, keepdims=True)
        s = jnp.var(v, axis=1, keepdims=True)
        return (v - m) / jnp.sqrt(s + eps)

    def _ln_t(v, eps=1e-05):
        m = jnp.mean(v, axis=-1, keepdims=True)
        s = jnp.var(v, axis=-1, keepdims=True)
        return (v - m) / jnp.sqrt(s + eps)

    def _to_tokens(v):
        B_, C_, H_, W_ = v.shape
        return v.reshape(B_, C_, H_ * W_).transpose(0, 2, 1)

    def _from_tokens(t, like):
        B_, C_, H_, W_ = like.shape
        return t.transpose(0, 2, 1).reshape(B_, C_, H_, W_)
    x = x + _L0_conv_ref(_gn(x), L0_conv_qkv_w, L0_conv_qkv_b, L0_conv_proj_w, L0_conv_proj_b, L0_conv_bias_table)
    x = x + _L1_conv_ref(_gn(x), L1_conv_value_proj_w, L1_conv_value_proj_b, L1_conv_offset_mask_w, L1_conv_offset_mask_b, L1_conv_output_proj_w, L1_conv_output_proj_b)
    return x

_drawn_inputs = setup_inputs


def setup_inputs(seed=0):
    import zlib

    import numpy as np

    out = dict(_drawn_inputs(seed))
    spreads = {'L1_conv_value_proj_b': (0.0, 0.1), 'L1_conv_output_proj_b': (0.0, 0.1)}
    factors = {'L0_conv_qkv_w': 8.0,
     'L0_conv_qkv_b': 8.0,
     'L0_conv_proj_w': 8.0,
     'L0_conv_bias_table': 8.0,
     'L0_conv_proj_b': 5.528}
    for name, (base, spread) in spreads.items():
        noise = np.random.default_rng([zlib.crc32(name.encode()), seed]).standard_normal(out[name].shape)
        drawn = base * np.exp(spread * noise) if base else spread * noise
        out[name] = jnp.asarray(drawn.astype(out[name].dtype))
    for name, factor in factors.items():
        out[name] = (out[name] * factor).astype(out[name].dtype)
    return out
```

```python
from contextlib import ExitStack

import concourse.bass as bass
from concourse import mybir

ALU = mybir.AluOpType
ACT = mybir.ActivationFunctionType
AX = mybir.AxisListType
F32 = mybir.dt.float32
BF16 = mybir.dt.bfloat16
I32 = mybir.dt.int32
U32 = mybir.dt.uint32

B, C, H, W = 2, 128, 128, 128
PIX = H * W
P = 128

WS = 16
NH = 8
HD = C // NH
NT = WS * WS
REL = 2 * WS - 1
PAIRS = B * (H // WS) * (W // WS) // 2
SLOTS = 2 * NH
TERMS = ((0, 0), (0, 1), (1, 0), (1, 1), (0, 2), (2, 0))
STACK = len(TERMS) * HD
VA = 32
SBIAS = 8
SCALE = float(HD) ** -0.5
T_LAG, READ_LAG = 2, 3
PV_LAG = 4
AHEAD = 2
GN_EPS = 1e-5
CHUNK = 4 * W


def wait(eng, sem, value):
    if isinstance(value, int) and value <= 0:
        return
    eng.wait_ge(sem, value)


def gate(eng, passed, sem, value):
    if isinstance(value, int) and value <= 0:
        return
    eng.wait_ge(sem, value)
    eng.sem_inc(passed, 1)


def group_matrix(nc, pool, ctx, mat, ready):
    v = mat[:].rearrange("p (j i) -> p j i", i=4)
    nc.gpsimd.memset(mat[:], 0.25).then_inc(ready, 1)
    pool.wait_ge(ready, 1)
    nc.gpsimd.affine_select(out=v, in_=v, compare_op=ALU.is_ge, fill=0.0, base=0,
                            pattern=[[-4, P // 4], [0, 4]], channel_multiplier=1).then_inc(ready, 1)
    pool.wait_ge(ready, 2)
    nc.gpsimd.affine_select(out=v, in_=v, compare_op=ALU.is_ge, fill=0.0, base=3,
                            pattern=[[4, P // 4], [0, 4]], channel_multiplier=-1).then_inc(ready, 1)


def identity_matrix(nc, pool, mat, ready):
    nc.gpsimd.memset(mat[:], 0.0).then_inc(ready, 1)
    pool.wait_ge(ready, 1)
    nc.gpsimd.affine_select(out=mat[:], in_=mat[:], compare_op=ALU.not_equal, fill=1.0, base=0,
                            pattern=[[-1, P]], channel_multiplier=1).then_inc(ready, 1)


def group_scales(nc, dve, moments, gst, gv, scale, shift, step, s0, part, p0, root, r0):
    nc.vector.tensor_copy(gst[:], moments).then_inc(step, 1)
    dve.wait_ge(step, s0 + 1)
    nc.vector.tensor_tensor(gv[:, 3:4], gst[:, 0:1], gst[:, 0:1], ALU.mult).then_inc(step, 1)
    dve.wait_ge(step, s0 + 2)
    nc.vector.tensor_tensor(gv[:, 2:3], gst[:, 1:2], gv[:, 3:4], ALU.subtract).then_inc(step, 1)
    dve.wait_ge(step, s0 + 3)
    nc.vector.tensor_scalar(gv[:, 0:1], gv[:, 2:3], GN_EPS, None, ALU.add).then_inc(part, 1)
    dve.wait_ge(root, r0 + 1)
    dve.wait_ge(part, p0 + 1)
    nc.vector.reciprocal(gv[:, 2:3], gv[:, 1:2]).then_inc(step, 1)
    dve.wait_ge(step, s0 + 4)
    nc.vector.tensor_tensor(gv[:, 3:4], gv[:, 2:3], gv[:, 2:3], ALU.mult).then_inc(step, 1)
    dve.wait_ge(step, s0 + 5)
    nc.vector.tensor_tensor(gv[:, 3:4], gv[:, 3:4], gv[:, 0:1], ALU.mult).then_inc(step, 1)
    dve.wait_ge(step, s0 + 6)
    nc.vector.tensor_scalar(gv[:, 3:4], gv[:, 3:4], -0.5, 1.5, ALU.mult, ALU.add).then_inc(step, 1)
    dve.wait_ge(step, s0 + 7)
    nc.vector.tensor_tensor(scale, gv[:, 2:3], gv[:, 3:4], ALU.mult).then_inc(step, 1)
    dve.wait_ge(step, s0 + 8)
    nc.vector.tensor_tensor(gv[:, 3:4], gst[:, 0:1], scale, ALU.mult).then_inc(step, 1)
    dve.wait_ge(step, s0 + 9)
    nc.vector.tensor_scalar(shift, gv[:, 3:4], -1.0, None, ALU.mult).then_inc(part, 1)


def attention(nc, x, w_qkv, b_qkv, bv_row, rel_rev, attended, rel_rows, parts_dram):
    with ExitStack() as ctx:
        def sb(name, shape, dt=F32):
            return ctx.enter_context(nc.sbuf_tensor(name, shape, dt))

        def sem(name):
            return ctx.enter_context(nc.semaphore(name))

        wqkv_sb = sb("wqkv_sb", [P, 3 * C])
        bqkv_sb = sb("bqkv_sb", [P, 3])
        bqn_sb = sb("bqn_sb", [P, 1])
        bv_sb = sb("bv_sb", [P, C])
        ident = sb("a_ident", [P, P])
        gmat = sb("a_gmat", [P, P])
        nbias = sb("nbias", [P, NH, 2, NT])
        stats_in = sb("a_stats_in", [P, 2, 2048])
        bn = sb("a_bn", [P, PIX // 512, 6])
        mv = sb("a_mv", [P, 2])
        ex = sb("a_ex", [P, 2])
        gst = sb("a_gst", [P, 2])
        gv = sb("a_gv", [P, 4])
        gn = sb("a_gn", [P, B, 2])
        gnp = sb("a_gnp", [P, 2])
        strips = sb("strips", [P, 2 * WS * W])
        xraw = sb("xraw", [P, 2 * NT])
        xn = sb("xn", [P, 2, 2 * NT])
        qk = sb("qk", [P, 2, 2 * NT])
        rest = sb("rest", [P, 2, 2 * NT])
        parts = sb("parts", [P, 3, 2, 2 * NT], BF16)
        stack = sb("stack", [STACK, 2, 2, NH, 2 * NT], BF16)
        va = sb("va", [P, 2, 4, NH, VA])
        sbias = sb("sbias", [P, SBIAS, 2, NT])
        nmax = sb("nmax", [P, SBIAS, 2])
        prob = sb("prob", [P, 4, 2, NT])
        probT = sb("probT", [P, 8, 2, NT])
        oT = sb("oT", [P, 2, 2 * NT])
        rsum = sb("rsum", [P, 2 * NH])
        on = sb("on", [P, 4, 2, C])

        s_ps = ctx.enter_context(nc.psum_tensor("s_ps", [P, 2, 2, NT], F32))
        pt_ps = ctx.enter_context(nc.psum_tensor("pt_ps", [P, 2, 2, NT], F32))
        o_ps = ctx.enter_context(nc.psum_tensor("o_ps", [P, 2, 2 * NT], F32))
        x_ps = ctx.enter_context(nc.psum_tensor("x_ps", [P, 2 * NH * VA], F32))
        qkv_ps = ctx.enter_context(nc.psum_tensor("qkv_ps", [P, 512], F32))
        x_view = x_ps[:].rearrange("p (a h c) -> p a h c", a=2, h=NH)

        weights_in = sem("weights_in")
        rows_out = sem("rows_out")
        bias_in = sem("bias_in")
        bias_neg = sem("bias_neg")
        bq_neg = sem("bq_neg")
        va_ones = sem("va_ones")
        id_ready = sem("id_ready")
        gmat_ready = sem("gmat_ready")
        st_in = [sem("st_in0"), sem("st_in1")]
        st_used = sem("st_used")
        gn_step = sem("gn_step")
        gn_sum = sem("gn_sum")
        gn_root = sem("gn_root")
        gn_ready = sem("gn_ready")
        chunk_in = [sem("chunk_in0"), sem("chunk_in1")]
        win_copied = sem("win_copied")
        gnp_ready = sem("gnp_ready")
        xn_ready = sem("xn_ready")
        q_done = sem("q_done")
        k_done = sem("k_done")
        v_done = sem("v_done")
        q_read = sem("q_read")
        k_read = sem("k_read")
        v_read = sem("v_read")
        split_step = sem("split_step")
        parts_out = sem("parts_out")
        stack_in = sem("stack_in")
        s_done = sem("s_done")
        max_done = sem("max_done")
        exp_done = sem("exp_done")
        t_done = sem("t_done")
        t_read_v = sem("t_read_v")
        t_read_a = sem("t_read_a")
        pv_done = sem("pv_done")
        recip_done = sem("recip_done")
        o_read = sem("o_read")
        x_done = sem("x_done")
        norm_done = sem("norm_done")
        y_out = [sem("y_out0"), sem("y_out1")]
        sp_passed = sem("sp_passed")
        pool_passed = sem("pool_passed")
        dve_passed = sem("dve_passed")

        block = ctx.enter_context(nc.Block())

        NSTAT = PIX // 2048
        x_chan = x.rearrange("b c h w -> b c (h w)")

        def token_rows(dram, p, w, half):
            strip = p // 4
            at = strip * (WS * W * C) + half * (NT // 2 // WS * W * C) + ((p % 4) * 2 + w) * (WS * C)
            return bass.AP(dram.tensor, dram.offset + at, [[W * C, NT // 2 // WS], [C, WS], [1, C]])

        @block.sync
        def _(sp):
            for t, src in ((wqkv_sb, w_qkv), (bqkv_sb, b_qkv)):
                sp.dma_start(t[:], src).then_inc(weights_in, 16)
            sp.dma_start(bv_sb[:], bv_row.partition_broadcast(P)).then_inc(weights_in, 16)
            for xq in range(WS):
                src = bass.AP(rel_rev.tensor, rel_rev.offset + WS - 1 - xq, [[REL, NH * REL], [1, WS]])
                dst = rel_rows[xq].rearrange("(r k) -> r k", k=WS)
                sp.dma_start(dst, src).then_inc(rows_out, 16)
            for b in range(B):
                for n in range(NSTAT):
                    i = b * NSTAT + n
                    if i >= 2:
                        sp.wait_ge(st_used, i - 1)
                    sp.dma_start(stats_in[:, i % 2, :], x_chan[b][:, n * 2048:(n + 1) * 2048]) \
                      .then_inc(st_in[i % 2], 16)
            sp.wait_ge(rows_out, 16 * WS)
            for yq in range(WS):
                half, row = yq // 8, yq % 8
                src = bass.AP(rel_rows.tensor, rel_rows.offset + (WS - 1 - yq) * WS,
                              [[NH * REL * WS, WS], [REL * WS, NH], [1, NT]])
                sp.dma_start(nbias[row * WS:(row + 1) * WS, :, half, :], src).then_inc(bias_in, 16)
            for n in range(6):
                if n >= 2:
                    sp.wait_ge(chunk_in[n % 2], 16 * (n // 2))
                sp.dma_start(strips[:, n * CHUNK:(n + 1) * CHUNK],
                             x_chan[0][:, n * CHUNK:(n + 1) * CHUNK]).then_inc(chunk_in[n % 2], 16)

            def store_parts(p, par):
                gate(sp, sp_passed, split_step, 4 * p + 4)
                wait(sp, stack_in, 16 * 2 * len(TERMS) * (p - 1))
                sp.dma_start(parts_dram[par], parts[:].rearrange("p a b n -> p (a b n)")).then_inc(parts_out, 16)

            def restack(p, par):
                gate(sp, sp_passed, parts_out, 16 * p + 16)
                wait(sp, s_done, SLOTS * (p - 1))
                for t, (tq, tk) in enumerate(TERMS):
                    for qk_i, part in ((0, tq), (1, tk)):
                        row = 3 * 2 * 2 * NT
                        src = bass.AP(parts_dram.tensor,
                                      parts_dram.offset + par * P * row + (part * 2 + qk_i) * 2 * NT,
                                      [[row, HD], [HD * row, NH], [1, 2 * NT]])
                        sp.dma_start(stack[t * HD:(t + 1) * HD, par, qk_i], src).then_inc(stack_in, 16)

            def store(p, w, par):
                sp.wait_ge(norm_done, 2 * (2 * p + w) + 2)
                for half in range(2):
                    sp.dma_start(token_rows(attended, p, w, half), on[:, 2 * par + w, half, :]) \
                      .then_inc(y_out[par], 16)

            def pair(p, par, first=False, left=AHEAD):
                if left == AHEAD:
                    sp.wait_ge(win_copied, p + 2)
                    sp.wait_ge(chunk_in[par], 16 * (p // 2 + 3))
                    q = (p + 6) % PAIRS
                    sp.dma_start(strips[:, bass.ds(((p + 6) % 8) * CHUNK, CHUNK)],
                                 bass.AP(x.tensor, x.offset + (q // 32) * (C * PIX) + (q % 32) * CHUNK,
                                         [[PIX, P], [1, CHUNK]])).then_inc(chunk_in[par], 16)
                if left >= 1:
                    restack(p + 1, 1 - par)
                if not first:
                    store(p - 1, 1, 1 - par)
                if left == AHEAD:
                    store_parts(p + 2, par)
                store(p, 0, par)

            store_parts(0, 0)
            restack(0, 0)
            store_parts(1, 1)
            pair(0, 0, first=True)
            with sp.Fori(0, (PAIRS - 4) // 2) as i:
                pair(2 * i + 1, 1)
                pair(2 * i + 2, 0)
            pair(PAIRS - 3, 1)
            pair(PAIRS - 2, 0, left=1)
            pair(PAIRS - 1, 1, left=0)
            store(PAIRS - 1, 1, 1)
            for par in range(2):
                sp.wait_ge(y_out[par], 64 * (PAIRS // 2))

        @block.gpsimd
        def _(pool):
            identity_matrix(nc, pool, ident, id_ready)
            group_matrix(nc, pool, ctx, gmat, gmat_ready)
            nc.gpsimd.memset(va[:], 0.0).then_inc(va_ones, 1)
            pool.wait_ge(va_ones, 1)
            nc.gpsimd.memset(va[:, :, :, :, HD:HD + 1], 1.0).then_inc(va_ones, 1)

            def normalise(p, par):
                pool.wait_ge(chunk_in[par], 16 * (p // 2 + 2))
                pool.wait_ge(chunk_in[1 - par], 16 * (p // 2 + 2 + par))
                src = strips[:, bass.ds(((p // 4) % 2) * (WS * W) + (p % 4) * 2 * WS, (WS - 1) * W + 2 * WS)]
                src = bass.AP(src.tensor, src.offset, [src.ap[0], [W, WS], [WS, 2], [1, WS]])
                dst = xraw[:].rearrange("p (w r c) -> p r w c", w=2, r=WS)
                gate(pool, pool_passed, xn_ready, p)
                nc.gpsimd.tensor_copy(dst, src).then_inc(win_copied, 1)
                nc.gpsimd.tensor_copy(gnp[:], gn[:, bass.ds(p // 32, 1), :]).then_inc(gnp_ready, 1)
                gate(pool, pool_passed, win_copied, p + 1)
                gate(pool, pool_passed, gnp_ready, p + 1)
                gate(pool, pool_passed, v_done, p - 1)
                nc.gpsimd.tensor_scalar(xn[:, par, :], xraw[:], gnp[:, 0:1], gnp[:, 1:2],
                                        ALU.mult, ALU.add).then_inc(xn_ready, 1)

            def split(p):
                pool.wait_ge(q_read, p + 1)
                pool.wait_ge(k_read, p + 1)
                gate(pool, pool_passed, parts_out, 16 * p)
                nc.gpsimd.tensor_copy(parts[:, 0], qk[:]).then_inc(split_step, 1)
                gate(pool, pool_passed, split_step, 4 * p + 1)
                nc.gpsimd.tensor_tensor(rest[:], qk[:], parts[:, 0], ALU.subtract).then_inc(split_step, 1)
                gate(pool, pool_passed, split_step, 4 * p + 2)
                nc.gpsimd.tensor_copy(parts[:, 1], rest[:]).then_inc(split_step, 1)
                gate(pool, pool_passed, split_step, 4 * p + 3)
                nc.gpsimd.tensor_tensor(parts[:, 2], rest[:], parts[:, 1], ALU.subtract).then_inc(split_step, 1)

            pool.wait_ge(gn_ready, 2 * B)
            normalise(0, 0)
            split(0)
            normalise(1, 1)
            split(1)
            with pool.Fori(0, (PAIRS - 2) // 2) as i:
                for par in range(2):
                    normalise(2 * i + 2 + par, par)
                    split(2 * i + 2 + par)

        @block.tensor
        def _(pe):
            pe.wait_ge(weights_in, 48)
            pe.wait_ge(id_ready, 2)
            pe.wait_ge(gmat_ready, 3)
            for b in range(B):
                pe.wait_ge(gn_step, 3 * b + 3)
                nc.tensor.matmul(x_ps[:, 0:2], gmat[:], ex[:], start=True, stop=True).then_inc(gn_sum, 1)

            def proj_q(p, par):
                pe.wait_ge(xn_ready, p + 1)
                wait(pe, k_read, p)
                wait(pe, v_read, p - 1)
                nc.tensor.matmul(qkv_ps[:], wqkv_sb[:, 0:C], xn[:, par, :], start=True, stop=True).then_inc(q_done, 1)

            def proj_k(p, par):
                pe.wait_ge(q_read, p + 1)
                nc.tensor.matmul(qkv_ps[:], wqkv_sb[:, C:2 * C], xn[:, par, :], start=True, stop=True) \
                  .then_inc(k_done, 1)

            def proj_v(p, par):
                pe.wait_ge(k_read, min(p + 2, PAIRS) if isinstance(p, int) else p + 2)
                for n in range(4):
                    mm = nc.tensor.matmul(qkv_ps[:, n * C:(n + 1) * C], xn[:, par, n * P:(n + 1) * P],
                                          wqkv_sb[:, 2 * C:3 * C], start=True, stop=True)
                mm.then_inc(v_done, 1)

            def scores(p, n, par):
                w, h = divmod(n, NH)
                if n == 0:
                    pe.wait_ge(stack_in, 16 * 2 * len(TERMS) * (p + 1))
                g = SLOTS * p + n
                wait(pe, max_done, g - 1)
                for half in range(2):
                    at = w * NT + half * P
                    mm = nc.tensor.matmul(s_ps[:, n % 2, half, :], stack[:, par, 0, h, at:at + P],
                                          stack[:, par, 1, h, w * NT:(w + 1) * NT], start=True, stop=True)
                mm.then_inc(s_done, 1)

            def turn(p, n):
                g = SLOTS * p + n
                pe.wait_ge(exp_done, g + 1)
                if n % 2 == 0:
                    wait(pe, t_read_a, NH * p + n // 2)
                else:
                    wait(pe, t_read_v, NH * p + n // 2)
                for half in range(2):
                    for kh in range(2):
                        mm = nc.tensor.transpose(pt_ps[:, n % 2, kh, half * P:(half + 1) * P],
                                                 prob[:, n % 4, half, kh * P:(kh + 1) * P], ident[:])
                mm.then_inc(t_done, 1)

            def weigh(p, k, par):
                w, t = divmod(k, 2)
                pe.wait_ge(t_read_a, NH * p + 2 * k + 2)
                pe.wait_ge(t_read_v, NH * p + 2 * k + 2)
                if k == 0:
                    pe.wait_ge(v_read, p + 1)
                if t == 0:
                    wait(pe, o_read, 2 * p + w - 1)
                for kh in range(2):
                    for j in range(4):
                        mm = nc.tensor.matmul(o_ps[32 * j:32 * j + VA, w, t * NT:(t + 1) * NT],
                                              va[:, par, 2 * w + kh, 4 * t + j, :],
                                              probT[:, (4 * k + j) % 8, kh, :], start=(kh == 0), stop=(kh == 1))
                mm.then_inc(pv_done, 1)

            def turn_out(win, w):
                pe.wait_ge(o_read, win + 1)
                wait(pe, norm_done, 2 * win)
                for half in range(2):
                    for t in range(2):
                        at = (2 * half + t) * P
                        mm = nc.tensor.transpose(x_ps[:, at:at + P], oT[:, w, t * NT + half * P:t * NT + (half + 1) * P],
                                                 ident[:])
                mm.then_inc(x_done, 1)

            def pair(p, par, first=False, left=AHEAD):
                for n in range(SLOTS):
                    scores(p, n, par)
                    if n >= T_LAG:
                        turn(p, n - T_LAG)
                    elif not first:
                        turn(p - 1, n - T_LAG + SLOTS)
                    if n % 4 == 3:
                        if n > 3:
                            weigh(p, (n - 7) // 4, par)
                        elif not first:
                            weigh(p - 1, 3, 1 - par)
                    if n == PV_LAG + 1 and not first:
                        turn_out(2 * p - 1, 1)
                    if n == NH + PV_LAG + 1:
                        turn_out(2 * p, 0)
                    if n == 0 and left == AHEAD:
                        proj_q(p + 2, par)
                    if n == 2 and left == AHEAD:
                        proj_k(p + 2, par)
                    if n == 4 and left >= 1:
                        proj_v(p + 1, 1 - par)

            proj_q(0, 0)
            proj_k(0, 0)
            proj_q(1, 1)
            proj_k(1, 1)
            proj_v(0, 0)
            pair(0, 0, first=True)
            with pe.Fori(0, (PAIRS - 4) // 2) as i:
                pair(2 * i + 1, 1)
                pair(2 * i + 2, 0)
            pair(PAIRS - 3, 1)
            pair(PAIRS - 2, 0, left=1)
            pair(PAIRS - 1, 1, left=0)
            turn(PAIRS - 1, SLOTS - 2)
            turn(PAIRS - 1, SLOTS - 1)
            weigh(PAIRS - 1, 3, 1)
            turn_out(2 * PAIRS - 1, 1)

        @block.scalar
        def _(act):
            for b in range(B):
                act.wait_ge(gn_ready, 2 * b + 1)
                nc.scalar.activation(gv[:, 1:2], gv[:, 0:1], ACT.Sqrt).then_inc(gn_root, 1)
            act.wait_ge(weights_in, 48)
            nc.scalar.mul(bqn_sb[:], bqkv_sb[:, 0:1], -SCALE).then_inc(bq_neg, 1)
            act.wait_ge(bq_neg, 1)

            def read_q(p):
                act.wait_ge(q_done, p + 1)
                wait(act, split_step, 4 * p)
                nc.scalar.activation(qk[:, 0, :], qkv_ps[:], ACT.Identity, bias=bqn_sb[:, 0:1],
                                     scale=-SCALE).then_inc(q_read, 1)

            def read_k(p):
                act.wait_ge(k_done, p + 1)
                nc.scalar.activation(qk[:, 1, :], qkv_ps[:], ACT.Identity, bias=bqkv_sb[:, 1:2]).then_inc(k_read, 1)

            def exp(p, n):
                g = SLOTS * p + n
                act.wait_ge(max_done, g + 1)
                wait(act, t_done, g - 3)
                for half in range(2):
                    ins = nc.scalar.activation(prob[:, n % 4, half, :], sbias[:, n % SBIAS, half, :], ACT.Exp,
                                               bias=nmax[:, n % SBIAS, half:half + 1], scale=-1.0)
                ins.then_inc(exp_done, 1)

            def read_turned(p, n):
                act.wait_ge(t_done, SLOTS * p + n + 1)
                wait(act, pv_done, 4 * p + n // 4 - 1)
                nc.scalar.copy(probT[:, n % 8], pt_ps[:, n % 2]).then_inc(t_read_a, 1)

            def read_o(win, w):
                act.wait_ge(pv_done, 2 * (win + 1))
                wait(act, x_done, win - 1)
                nc.scalar.copy(oT[:, w], o_ps[:, w]).then_inc(o_read, 1)

            def pair(p, first=False, left=AHEAD):
                for n in range(SLOTS):
                    exp(p, n)
                    m = n - READ_LAG
                    if m % 2 == 0 and not (first and m < 0):
                        read_turned(p if m >= 0 else p - 1, m % SLOTS)
                    if n == PV_LAG and not first:
                        read_o(2 * p - 1, 1)
                    if n == NH + PV_LAG:
                        read_o(2 * p, 0)
                    if n == 1 and left == AHEAD:
                        read_q(p + 2)
                    if n == 3 and left == AHEAD:
                        read_k(p + 2)

            for p in range(AHEAD):
                read_q(p)
                read_k(p)
            pair(0, first=True)
            with act.Fori(0, (PAIRS - 4) // 2) as i:
                pair(2 * i + 1)
                pair(2 * i + 2)
            pair(PAIRS - 3)
            pair(PAIRS - 2, left=1)
            pair(PAIRS - 1, left=0)
            read_turned(PAIRS - 1, SLOTS - 2)
            read_o(2 * PAIRS - 1, 1)

        @block.vector
        def _(dve):
            for b in range(B):
                for n in range(NSTAT):
                    i = b * NSTAT + n
                    dve.wait_ge(st_in[i % 2], 16 * (i // 2 + 1))
                    for m in range(4):
                        ins = nc.vector.bn_stats(bn[:, 4 * n + m, :], stats_in[:, i % 2, m * 512:(m + 1) * 512])
                    ins.then_inc(st_used, 1)
                dve.wait_ge(st_used, NSTAT * (b + 1))
                nc.vector.bn_aggr(mv[:], bn[:].rearrange("p a b -> p (a b)")).then_inc(gn_step, 1)
                dve.wait_ge(gn_step, 3 * b + 1)
                nc.vector.tensor_copy(ex[:, 0:1], mv[:, 0:1]).then_inc(gn_step, 1)
                nc.vector.scalar_tensor_tensor(out=ex[:, 1:2], in0=mv[:, 0:1], scalar=mv[:, 0:1], in1=mv[:, 1:2],
                                               op0=ALU.mult, op1=ALU.add).then_inc(gn_step, 1)
                dve.wait_ge(gn_sum, b + 1)
                group_scales(nc, dve, x_ps[:, 0:2], gst, gv, gn[:, b, 0:1], gn[:, b, 1:2], recip_done, 9 * b,
                             gn_ready, 2 * b, gn_root, b)
            RB = 9 * B
            dve.wait_ge(bias_in, 16 * WS)
            nc.vector.tensor_scalar(nbias[:].rearrange("p h a k -> p (h a k)"),
                                    nbias[:].rearrange("p h a k -> p (h a k)"), -1.0, None,
                                    ALU.mult).then_inc(bias_neg, 1)
            dve.wait_ge(bias_neg, 1)
            dve.wait_ge(va_ones, 2)
            dve.wait_ge(weights_in, 48)

            def read_v(p, par):
                dve.wait_ge(v_done, p + 1)
                wait(dve, pv_done, 4 * (p - 1))
                nc.vector.tensor_tensor(va[:, par, :, :, 0:HD],
                                        qkv_ps[:].rearrange("p (n h c) -> p n h c", n=4, h=NH),
                                        bv_sb[:].rearrange("p (h c) -> p h c", h=NH).unsqueeze(1)
                                        .to_broadcast([P, 4, NH, HD]),
                                        ALU.add).then_inc(v_read, 1)

            def bias_max(p, n):
                g = SLOTS * p + n
                h = n % NH
                gate(dve, dve_passed, s_done, g + 1)
                for half in range(2):
                    ins = nc.vector.tensor_tensor_reduce(
                        out=sbias[:, n % SBIAS, half, :], in0=s_ps[:, n % 2, half, :], in1=nbias[:, h, half, :],
                        scale=1.0, scalar=3.0e38, op0=ALU.add, op1=ALU.min,
                        accum_out=nmax[:, n % SBIAS, half:half + 1])
                ins.then_inc(max_done, 1)

            def read_turned(p, n):
                dve.wait_ge(t_done, SLOTS * p + n + 1)
                wait(dve, pv_done, 4 * p + n // 4 - 1)
                nc.vector.tensor_copy(probT[:, n % 8], pt_ps[:, n % 2]).then_inc(t_read_v, 1)

            def norm(win, w, par, k):
                dve.wait_ge(x_done, win + 1)
                wait(dve, norm_done, 2 * win)
                nc.vector.reciprocal(rsum[:].rearrange("p (a h) -> p a h", h=NH),
                                     x_view[:, :, :, HD]).then_inc(recip_done, 1)
                dve.wait_ge(recip_done, RB + win + 1)
                wait(dve, y_out[par], 64 * k)
                for half in range(2):
                    nc.vector.tensor_tensor(on[:, 2 * par + w, half, :].rearrange("p (h c) -> p h c", h=NH),
                                            x_view[:, half, :, 0:HD],
                                            rsum[:, half * NH:(half + 1) * NH].unsqueeze(2)
                                            .to_broadcast([P, NH, HD]), ALU.mult).then_inc(norm_done, 1)

            def pair(p, par, first=False, left=AHEAD):
                for n in range(SLOTS):
                    bias_max(p, n)
                    m = n - READ_LAG
                    if m % 2 == 1 and not (first and m < 0):
                        read_turned(p if m >= 0 else p - 1, m % SLOTS)
                    if n == PV_LAG + 2 and not first:
                        norm(2 * p - 1, 1, 1 - par, (p - 1) // 2)
                    if n == NH + PV_LAG + 2:
                        norm(2 * p, 0, par, p // 2)
                    if n == 5 and left >= 1:
                        read_v(p + 1, 1 - par)

            read_v(0, 0)
            pair(0, 0, first=True)
            with dve.Fori(0, (PAIRS - 4) // 2) as i:
                pair(2 * i + 1, 1)
                pair(2 * i + 2, 0)
            pair(PAIRS - 3, 1)
            pair(PAIRS - 2, 0, left=1)
            pair(PAIRS - 1, 1, left=0)
            for m in range(SLOTS - READ_LAG, SLOTS):
                if m % 2 == 1:
                    read_turned(PAIRS - 1, m)
            norm(2 * PAIRS - 1, 1, 1, (PAIRS - 1) // 2)


KS = 3
K2 = KS * KS
G = 8
CG = C // G
OM = 3 * K2 * G
KG = K2 * G
TAPS = KS + 2
PAD = TAPS // 2
XP = W + 2 * PAD + 3
YP = H + 2 * PAD
COLS = 4
GROUPS = W // COLS
RING = 8
AHEAD_V = RING - 1
MAX_BITS = 0x7F800000


def deformable(nc, x, attended, w_proj, bproj_row, w_value, bv_row, w_om, bom_row, w_out, b_out, vals, out):
    with ExitStack() as ctx:
        def sb(name, shape, dt=F32):
            return ctx.enter_context(nc.sbuf_tensor(name, shape, dt))

        def sem(name):
            return ctx.enter_context(nc.semaphore(name))

        wproj_sb = sb("wproj_sb", [P, C])
        bproj_sb = sb("bproj_sb", [P, W])
        wvalue_sb = sb("wvalue_sb", [P, C])
        bvalue_sb = sb("bvalue_sb", [P, C])
        wom_sb = sb("wom_sb", [P, OM])
        bom_sb = sb("bom_sb", [P, OM])
        wout_sb = sb("wout_sb", [P, C])
        bout_sb = sb("bout_sb", [P, 1])
        ident = sb("d_ident", [P, P])
        gmat = sb("d_gmat", [P, P])
        ones = sb("ones", [P, 1], BF16)
        zeros = sb("zeros", [P, 1056])
        one_col = sb("one_col", [P, 2])
        x1 = sb("x1", [P, PIX])
        att = sb("att", [P, 2, COLS, C])
        bn = sb("d_bn", [P, PIX // 512, 6])
        mv = sb("d_mv", [P, 2])
        ex = sb("d_ex", [P, 2])
        gst = sb("d_gst", [P, 2])
        gv = sb("d_gv", [P, 4])
        gn = sb("d_gn", [P, 2])
        xn = sb("d_xn", [P, 2, COLS, H])
        vrow = sb("vrow", [P, 2, COLS, C])
        vring = sb("vring", [P, RING, TAPS * C])
        off = sb("off", [P, 2, COLS, OM])
        dist = sb("dist", [P, 3, COLS, 2 * KG])
        hat = sb("hat", [P, 3, COLS, 2 * KG])
        near = sb("near", [P, COLS, 2 * KG])
        inside = sb("inside", [P, COLS, KG])
        flag = sb("flag", [P, COLS, KG], BF16)
        mf = sb("mf", [P, 2, COLS, KG])
        my = sb("my", [P, 3, COLS, KG])
        tt = sb("tt", [P, 3, 3, COLS, KG])
        wt = sb("wt", [P, 2, COLS, TAPS, TAPS * G])
        prod = sb("prod", [P, 2, TAPS, TAPS * C])
        corr = sb("corr", [P, 2, COLS, C])
        ssum = sb("ssum", [P, COLS, C])
        sT = sb("sT", [P, COLS * H])
        cnt = sb("cnt", [1, 2, COLS * KG])
        cntk = sb("cntk", [1, 2, COLS * K2])
        cntr = sb("cntr", [1, 2, COLS])
        ib = sb("ib", [P, 2 * KG], I32)
        base0 = sb("base0", [P, 2 * KG])
        colx = sb("colx", [P, W])
        icol = sb("icol", [P, W], I32)
        origin = sb("origin", [P, KG])
        xs = sb("xs", [P, 1])
        loc = sb("loc", [P, 2 * KG])
        loci = sb("loci", [P, 2 * KG], I32)
        locf = sb("locf", [P, 2 * KG])
        gap = sb("gap", [P, 2 * KG])
        frac = sb("frac", [P, 2 * KG])
        comp = sb("comp", [P, 2 * KG])
        mfar = sb("mfar", [P, 3, KG])
        w4 = sb("w4", [P, 4, KG])
        idxf = sb("idxf", [P, 2, KG])
        idx = sb("idx", [P, KG], I32)
        idx1 = sb("idx1", [P, 1], I32)
        w41 = sb("w41", [P, 4])
        gath = sb("gath", [P, 4, CG])
        gsum = sb("gsum", [P, 3, CG])

        om_ps = ctx.enter_context(nc.psum_tensor("om_ps", [P, 2, 512], F32))
        sum_ps = ctx.enter_context(nc.psum_tensor("sum_ps", [P, 2, COLS * C], F32))
        t_ps = ctx.enter_context(nc.psum_tensor("t_ps", [P, COLS * H], F32))
        out_ps = ctx.enter_context(nc.psum_tensor("out_ps", [P, COLS * H], F32))
        cnt_ps = ctx.enter_context(nc.psum_tensor("cnt_ps", [P, 512], F32))
        a_ps = ctx.enter_context(nc.psum_tensor("a_ps", [P, 512], F32))

        w_in = sem("w_in")
        pad_out = sem("pad_out")
        consts = sem("consts")
        ones_ready = sem("ones_ready")
        zeros_ready = sem("zeros_ready")
        d_id = sem("d_id")
        d_gm = sem("d_gm")
        x_in = sem("x_in")
        att_in = [sem("att_in0"), sem("att_in1")]
        a_done = sem("a_done")
        b_added = sem("b_added")
        x1_ready = sem("x1_ready")
        g_step = sem("g_step")
        g_sum = sem("g_sum")
        g_root = sem("g_root")
        g_sq = sem("g_sq")
        vn_ready = sem("vn_ready")
        v_done = sem("dv_done")
        vrow_ready = sem("vrow_ready")
        vrow_out = [sem("vrow_out0"), sem("vrow_out1")]
        v_in = [sem("v_in0"), sem("v_in1")]
        xn_ready = sem("dxn_ready")
        om_done = sem("om_done")
        off_ready = sem("off_ready")
        dist_ready = sem("dist_ready")
        hat_ready = sem("hat_ready")
        near_step = sem("near_step")
        flag_ready = sem("flag_ready")
        cnt_done = sem("cnt_done")
        cnt_ready = sem("cnt_ready")
        coef_step = sem("coef_step")
        wt_ready = sem("wt_ready")
        prod_ready = sem("prod_ready")
        sum_done = sem("sum_done")
        corr_zero = sem("corr_zero")
        corr_ready = sem("corr_ready")
        ssum_ready = sem("ssum_ready")
        t_done = sem("dt_done")
        sT_ready = sem("sT_ready")
        out_done = sem("out_done")
        res_ready = sem("res_ready")
        stored = sem("stored")
        sp_passed = sem("d_sp_passed")
        pool_passed = sem("d_pool_passed")
        dve_passed = sem("d_dve_passed")
        far_step = sem("far_step")
        pick_step = sem("pick_step")
        gathered = sem("gathered")

        block = ctx.enter_context(nc.Block())

        x_chan = x.rearrange("b c h w -> b c (h w)")
        out_chan = out.rearrange("b c h w -> b c (h w)")
        QUARTER = PIX // 4
        cols = x1[:].rearrange("p (y x) -> p x y", x=W)
        NA = H // COLS
        LOADS = ((W + AHEAD_V + 1) // 2, (W + AHEAD_V) // 2)

        def at(dram, offset, dims):
            return bass.AP(dram.tensor, dram.offset + offset, dims)

        @block.sync
        def _(sp):
            for t, src in ((wproj_sb, w_proj), (wvalue_sb, w_value), (wom_sb, w_om), (wout_sb, w_out),
                           (bout_sb, b_out)):
                sp.dma_start(t[:], src).then_inc(w_in, 16)
            for t, src in ((bproj_sb, bproj_row), (bvalue_sb, bv_row), (bom_sb, bom_row)):
                sp.dma_start(t[:], src.partition_broadcast(P)).then_inc(w_in, 16)
            sp.wait_ge(zeros_ready, 1)
            for col in (*range(PAD), *range(PAD + W, XP)):
                sp.dma_start(at(vals, col * YP * C, [[YP * C // 16, 16], [1, YP * C // 16]]),
                             zeros[0:16, :]).then_inc(pad_out, 16)
            for row in (0, PAD + H):
                sp.dma_start(at(vals, (PAD * YP + row) * C, [[YP * C, W], [1, PAD * C]]),
                             zeros[:, 0:PAD * C]).then_inc(pad_out, 16)
            NPAD = XP - W + 2
            sp.wait_ge(pad_out, 16 * NPAD)

            with sp.Fori(0, B) as b:
                sp.wait_ge(stored, 64 * b)
                for n in range(4):
                    sp.dma_start(x1[:, n * QUARTER:(n + 1) * QUARTER],
                                 at(x, b * (C * PIX) + n * QUARTER, [[PIX, P], [1, QUARTER]])).then_inc(x_in, 16)
                with sp.Fori(0, NA // 2) as i:
                    for par in range(2):
                        a = b * NA + 2 * i + par
                        gate(sp, sp_passed, a_done, a)
                        gate(sp, sp_passed, att_in[par], 8 * (a - par))
                        sp.dma_start(att[:, par], at(attended, a * (COLS * W * C), [[C, P], [W * C, COLS], [1, C]])) \
                          .then_inc(att_in[par], 16)
                with sp.Fori(0, GROUPS // 2) as i:
                    for par in range(2):
                        v = b * GROUPS + 2 * i + par
                        sp.wait_ge(vrow_ready, v + 1)
                        sp.dma_start(at(vals, ((PAD + (2 * i + par) * COLS) * YP + PAD) * C,
                                        [[C, P], [YP * C, COLS], [1, C]]), vrow[:, par]).then_inc(vrow_out[par], 16)
                for par in range(2):
                    sp.wait_ge(vrow_out[par], (b + 1) * (8 * GROUPS))

                def load_column(n, slot, earlier):
                    sp.wait_ge(v_in[slot % 2], 16 * earlier)
                    sp.dma_start(vring[:, slot], at(vals, n * (YP * C), [[C, P], [1, TAPS * C]])) \
                      .then_inc(v_in[slot % 2], 16)

                for n in range(AHEAD_V):
                    load_column(n, n, b * LOADS[n % 2] + n // 2)
                with sp.Fori(0, W // RING) as i:
                    for c in range(RING):
                        sp.wait_ge(prod_ready, b * W + RING * i + c)
                        load_column(RING * i + c + AHEAD_V, (c + AHEAD_V) % RING,
                                    b * LOADS[(c + AHEAD_V) % 2] + RING // 2 * i + (c + AHEAD_V) // 2)
                sp.wait_ge(res_ready, (b + 1) * GROUPS)
                for n in range(4):
                    sp.dma_start(at(out, b * (C * PIX) + n * QUARTER, [[PIX, P], [1, QUARTER]]),
                                 x1[:, n * QUARTER:(n + 1) * QUARTER]).then_inc(stored, 16)
            sp.wait_ge(stored, 64 * B)

        @block.gpsimd
        def _(pool):
            nc.gpsimd.memset(zeros[:], 0.0).then_inc(zeros_ready, 1)
            nc.gpsimd.memset(ones[:], 1.0).then_inc(ones_ready, 1)
            nc.gpsimd.memset(one_col[:, 0:1], 1.0).then_inc(ones_ready, 1)
            nc.gpsimd.memset(one_col[:, 1:2], -1.0).then_inc(ones_ready, 1)
            identity_matrix(nc, pool, ident, d_id)
            group_matrix(nc, pool, ctx, gmat, d_gm)
            n_const = 0
            for dst, src, pattern, base, mult in (
                    (base0[:, 0:KG], ib[:, 0:KG], [[1, KS], [0, KS], [0, G]], -1, 0),
                    (base0[:, KG:], ib[:, KG:], [[0, KS], [1, KS], [0, G]], -1, 1),
                    (colx[:], icol[:], [[1, W]], 0, 0),
                    (origin[:], idx[:], [[0, K2], [1, G]], (PAD * YP + PAD) * G, 0)):
                nc.gpsimd.iota(src, pattern=pattern, base=base, channel_multiplier=mult).then_inc(consts, 1)
                pool.wait_ge(consts, n_const + 1)
                nc.gpsimd.tensor_copy(dst, src).then_inc(consts, 1)
                pool.wait_ge(consts, n_const + 2)
                n_const += 2
            pool.wait_ge(w_in, 16 * 8)
            pool.sem_inc(corr_ready, 1)
            n_gathered = pool.alloc_register("n_gathered")
            pool.reg_mov(n_gathered, 0)
            with pool.Fori(0, B) as b:
                gate(pool, pool_passed, x_in, 64 * (b + 1))
                with pool.Fori(0, NA) as i:
                    rows = x1[:, bass.ds(i * (COLS * W), COLS * W)].rearrange("p (r w) -> p r w", w=W)
                    nc.gpsimd.tensor_tensor(rows, rows, bproj_sb[:].unsqueeze(1).to_broadcast([P, COLS, W]),
                                            ALU.add).then_inc(b_added, 1)

                def far_weights(q, par, r):
                    n = [0]

                    def then(ins):
                        n[0] += 1
                        ins.then_inc(far_step, 1)
                        pool.wait_ge(far_step, n[0])

                    pool.sem_clear(far_step)
                    o = off[:, par, r]
                    then(nc.gpsimd.tensor_copy(xs[:], colx[:, bass.ds(q * COLS + r, 1)]))
                    then(nc.gpsimd.tensor_scalar(gap[:, 0:KG], base0[:, 0:KG], xs[:, 0:1], None, ALU.add))
                    then(nc.gpsimd.tensor_tensor(loc[:, 0:KG], gap[:, 0:KG], o[:, 0:KG], ALU.add))
                    then(nc.gpsimd.tensor_tensor(loc[:, KG:], base0[:, KG:], o[:, KG:2 * KG], ALU.add))
                    then(nc.gpsimd.tensor_scalar(loc[:], loc[:], -1.0, float(W), ALU.max, ALU.min))
                    then(nc.gpsimd.tensor_copy(loci[:], loc[:]))
                    then(nc.gpsimd.tensor_copy(locf[:], loci[:]))
                    then(nc.gpsimd.tensor_tensor(gap[:], locf[:], loc[:], ALU.subtract))
                    then(nc.gpsimd.tensor_scalar(gap[:], gap[:], 0.0, None, ALU.is_gt))
                    then(nc.gpsimd.tensor_tensor(locf[:], locf[:], gap[:], ALU.subtract))
                    then(nc.gpsimd.tensor_tensor(frac[:], loc[:], locf[:], ALU.subtract))
                    then(nc.gpsimd.tensor_scalar(comp[:], frac[:], -1.0, 1.0, ALU.mult, ALU.add))
                    then(nc.gpsimd.tensor_tensor(mfar[:, 0], o[:, 2 * KG:], mf[:, par, r], ALU.subtract))
                    then(nc.gpsimd.tensor_tensor(mfar[:, 1], comp[:, KG:], mfar[:, 0], ALU.mult))
                    then(nc.gpsimd.tensor_tensor(mfar[:, 2], frac[:, KG:], mfar[:, 0], ALU.mult))
                    for i, (side, row) in enumerate(((comp, 1), (comp, 2), (frac, 1), (frac, 2))):
                        then(nc.gpsimd.tensor_tensor(w4[:, i], side[:, 0:KG], mfar[:, row], ALU.mult))
                    then(nc.gpsimd.tensor_scalar(idxf[:, 0], locf[:, 0:KG], float(YP * G), None, ALU.mult))
                    then(nc.gpsimd.tensor_scalar(idxf[:, 1], locf[:, KG:], float(G), None, ALU.mult))
                    then(nc.gpsimd.tensor_tensor(idxf[:, 0], idxf[:, 0], idxf[:, 1], ALU.add))
                    then(nc.gpsimd.tensor_tensor(idxf[:, 0], idxf[:, 0], origin[:], ALU.add))
                    then(nc.gpsimd.tensor_copy(idx[:], idxf[:, 0]))

                def far_sample(par, r, j, g):
                    pool.sem_clear(pick_step)
                    nc.gpsimd.tensor_copy(idx1[:], idx[:, bass.ds(j, 1)]).then_inc(pick_step, 1)
                    nc.gpsimd.tensor_copy(w41[:].unsqueeze(2), w4[:, :, bass.ds(j, 1)]).then_inc(pick_step, 1)
                    pool.wait_ge(pick_step, 2)
                    for i, (dx, dy) in enumerate(((0, 0), (0, 1), (1, 0), (1, 1))):
                        pool.indirect_dma_start(
                            out=gath[:, i, :], out_offset=None, in_=vals_rows,
                            in_offset=bass.IndirectOffsetOnAxis(ap=idx1[:].bitcast(U32), axis=0),
                            element_offset=(dx * YP + dy) * C).then_inc(gathered, 16)
                    pool.reg_add(n_gathered, n_gathered, 64)
                    pool.wait_ge(gathered, n_gathered)
                    nc.gpsimd.tensor_tensor(gath[:], gath[:], w41[:].unsqueeze(2).to_broadcast([P, 4, CG]),
                                            ALU.mult).then_inc(pick_step, 1)
                    pool.wait_ge(pick_step, 3)
                    nc.gpsimd.tensor_tensor(gsum[:, 0:2], gath[:, 0:2], gath[:, 2:4], ALU.add).then_inc(pick_step, 1)
                    pool.wait_ge(pick_step, 4)
                    nc.gpsimd.tensor_tensor(gsum[:, 2], gsum[:, 0], gsum[:, 1], ALU.add).then_inc(pick_step, 1)
                    pool.wait_ge(pick_step, 5)
                    acc = corr[:, par, r, bass.ds(g * CG, CG)]
                    nc.gpsimd.tensor_tensor(acc, acc, gsum[:, 2], ALU.add).then_inc(pick_step, 1)
                    pool.wait_ge(pick_step, 6)

                def load_count(counts, par, at):
                    return pool.value_load(counts[0:1, par, bass.ds(at, 1)].bitcast(I32), min_val=0,
                                           max_val=MAX_BITS)

                vals_rows = vals.rearrange("x y (g c) -> (x y g) c", c=CG)
                with pool.Fori(0, GROUPS // 2) as i:
                    for par in range(2):
                        q = 2 * i + par
                        n = b * GROUPS + q
                        gate(pool, pool_passed, ssum_ready, n)
                        nc.gpsimd.memset(corr[:, par], 0.0).then_inc(corr_zero, 1)
                        pool.wait_ge(corr_zero, n + 1)
                        gate(pool, pool_passed, cnt_ready, 3 * n + 3)
                        for r in range(COLS):
                            any_far = load_count(cntr, par, r)
                            with pool.If(any_far > 0):
                                far_weights(q, par, r)
                                with pool.Fori(0, K2) as k:
                                    far_k = load_count(cntk, par, r * K2 + k)
                                    with pool.If(far_k > 0):
                                        with pool.Fori(0, G) as g:
                                            far_kg = load_count(cnt, par, r * KG + k * G + g)
                                            with pool.If(far_kg > 0):
                                                far_sample(par, r, k * G + g, g)
                        pool.sem_inc(corr_ready, 1)

        @block.tensor
        def _(pe):
            pe.wait_ge(w_in, 16 * 8)
            pe.wait_ge(d_id, 2)
            pe.wait_ge(d_gm, 3)
            pe.wait_ge(ones_ready, 3)
            for ahead in (a_done, v_done, sum_done):
                pe.sem_inc(ahead, 1)
            with pe.Fori(0, B) as b:
                with pe.Fori(0, NA // 2) as i:
                    for par in range(2):
                        a = b * NA + 2 * i + par
                        pe.wait_ge(att_in[par], 8 * (a - par) + 16)
                        pe.wait_ge(x1_ready, 2 * a)
                        for r in range(COLS):
                            mm = nc.tensor.matmul(a_ps[:, r * W:(r + 1) * W], att[:, par, r, :], wproj_sb[:],
                                                  start=True, stop=True)
                        mm.then_inc(a_done, 1)
                pe.wait_ge(g_step, 3 * b + 3)
                nc.tensor.matmul(a_ps[:, 0:2], gmat[:], ex[:], start=True, stop=True).then_inc(g_sum, 1)
                with pe.Fori(0, GROUPS // 2) as i:
                    for par in range(2):
                        v = b * GROUPS + 2 * i + par
                        pe.wait_ge(vn_ready, v + 1)
                        pe.wait_ge(vrow_ready, v)
                        for r in range(COLS):
                            mm = nc.tensor.matmul(a_ps[:, r * C:(r + 1) * C], xn[:, par, r, :], wvalue_sb[:],
                                                  start=True, stop=True)
                        mm.then_inc(v_done, 1)

                def offsets(q, par):
                    n = b * GROUPS + q
                    pe.wait_ge(xn_ready, n + 1)
                    pe.wait_ge(off_ready, 2 * n)
                    for r in range(COLS):
                        mm = nc.tensor.matmul(om_ps[:, r // 2, (r % 2) * OM:(r % 2 + 1) * OM], xn[:, par, r, :],
                                              wom_sb[:], start=True, stop=True)
                    mm.then_inc(om_done, 1)

                def count(q):
                    n = b * GROUPS + q
                    pe.wait_ge(flag_ready, n + 1)
                    pe.wait_ge(cnt_ready, 3 * n)
                    nc.tensor.matmul(cnt_ps[0:1, 0:COLS * KG], ones[:], flag[:].rearrange("p r k -> p (r k)"),
                                     start=True, stop=True).then_inc(cnt_done, 1)

                def taps(q, par, r):
                    n = b * W + q * COLS + r
                    pe.wait_ge(prod_ready, n + 1)
                    if r == 0:
                        pe.wait_ge(ssum_ready, b * GROUPS + q)
                    for dx in range(TAPS):
                        for dy in range(TAPS):
                            mm = nc.tensor.matmul(sum_ps[:, par, r * C:(r + 1) * C], ident[:],
                                                  prod[:, r % 2, dx, dy * C:(dy + 1) * C],
                                                  start=(dx + dy == 0), stop=(dx + dy == 2 * TAPS - 2))
                    mm.then_inc(sum_done, 1)

                def turn(q):
                    n = b * GROUPS + q
                    pe.wait_ge(ssum_ready, n + 2)
                    pe.wait_ge(sT_ready, n)
                    for r in range(COLS):
                        mm = nc.tensor.transpose(t_ps[:, r * H:(r + 1) * H], ssum[:, r, :], ident[:])
                    mm.then_inc(t_done, 1)

                def project(q):
                    n = b * GROUPS + q
                    pe.wait_ge(sT_ready, n + 1)
                    pe.wait_ge(res_ready, n)
                    nc.tensor.matmul(out_ps[:], wout_sb[:], sT[:], start=True, stop=True).then_inc(out_done, 1)

                def group(q, par, first=False, last=False):
                    for r in range(COLS):
                        taps(q, par, r)
                        if r == 0 and not last:
                            offsets(q + 1, 1 - par)
                        if r == 1 and not first:
                            turn(q - 1)
                        if r == 2 and not last:
                            count(q + 1)
                        if r == 2 and not first:
                            project(q - 1)

                offsets(0, 0)
                count(0)
                group(0, 0, first=True)
                with pe.Fori(0, (GROUPS - 2) // 2) as i:
                    group(2 * i + 1, 1)
                    group(2 * i + 2, 0)
                group(GROUPS - 1, 1, last=True)
                turn(GROUPS - 1)
                project(GROUPS - 1)

        @block.scalar
        def _(act):
            act.wait_ge(ones_ready, 3)
            with act.Fori(0, B) as b:
                act.wait_ge(g_sq, 2 * b + 1)
                nc.scalar.activation(gv[:, 1:2], gv[:, 0:1], ACT.Sqrt).then_inc(g_root, 1)
                act.wait_ge(g_sq, 2 * b + 2)
                with act.Fori(0, GROUPS // 2) as i:
                    for par in range(2):
                        v = b * GROUPS + 2 * i + par
                        act.wait_ge(v_done, v)
                        nc.scalar.activation(xn[:, par], cols[:, bass.ds((2 * i + par) * COLS, COLS), :],
                                             ACT.Identity, bias=gn[:, 1:2], scale=gn[:, 0:1]).then_inc(vn_ready, 1)
                act.wait_ge(v_done, (b + 1) * GROUPS + 1)

                def normalise(q, par, older):
                    act.wait_ge(om_done, older)
                    src = cols[:, q * COLS:(q + 1) * COLS, :] if isinstance(q, int) else \
                        cols[:, bass.ds(q * COLS, COLS), :]
                    nc.scalar.activation(xn[:, par], src, ACT.Identity, bias=gn[:, 1:2],
                                         scale=gn[:, 0:1]).then_inc(xn_ready, 1)

                def hats(q, par):
                    n = b * GROUPS + q
                    act.wait_ge(off_ready, 2 * n + 2)
                    act.wait_ge(near_step, 3 * n)
                    o = off[:, par, :, 0:2 * KG]
                    nc.scalar.activation(dist[:, 0], o, ACT.Abs, bias=one_col[:, 0:1]).then_inc(dist_ready, 1)
                    nc.scalar.activation(dist[:, 1], o, ACT.Abs).then_inc(dist_ready, 1)
                    nc.scalar.activation(dist[:, 2], o, ACT.Abs, bias=one_col[:, 1:2]).then_inc(dist_ready, 1)
                    act.wait_ge(wt_ready, n)
                    for j in range(3):
                        act.wait_ge(dist_ready, 3 * n + 1 + j)
                        nc.scalar.activation(hat[:, j], dist[:, j], ACT.Relu, bias=one_col[:, 0:1],
                                             scale=-1.0).then_inc(hat_ready, 1)

                def read_turned(q):
                    n = b * GROUPS + q
                    act.wait_ge(t_done, n + 1)
                    act.wait_ge(out_done, n)
                    nc.scalar.copy(sT[:], t_ps[:]).then_inc(sT_ready, 1)

                def group(q, par, first=False, left=2):
                    if left >= 2:
                        normalise(q + 2, par, b * GROUPS + q + 1)
                    if left >= 1:
                        hats(q + 1, 1 - par)
                    if not first:
                        read_turned(q - 1)

                normalise(0, 0, b * GROUPS)
                normalise(1, 1, b * GROUPS)
                hats(0, 0)
                group(0, 0, first=True)
                with act.Fori(0, (GROUPS - 4) // 2) as i:
                    group(2 * i + 1, 1)
                    group(2 * i + 2, 0)
                group(GROUPS - 3, 1)
                group(GROUPS - 2, 0, left=1)
                group(GROUPS - 1, 1, left=0)
                read_turned(GROUPS - 1)

        @block.vector
        def _(dve):
            dve.wait_ge(w_in, 16 * 8)
            NORM, STEPS = 9, 13
            dve.sem_inc(ssum_ready, 1)
            with dve.Fori(0, B) as b:
                with dve.Fori(0, NA // 2) as i:
                    for par in range(2):
                        ai = 2 * i + par
                        a = b * NA + ai
                        dve.wait_ge(a_done, a + 2)
                        dve.wait_ge(b_added, a + 1)
                        rows = x1[:, bass.ds(ai * (COLS * W), COLS * W)]
                        nc.vector.tensor_tensor(rows, a_ps[:], rows, ALU.add).then_inc(x1_ready, 1)
                        dve.wait_ge(x1_ready, 2 * a + 1)
                        nc.vector.bn_stats(bn[:, bass.ds(ai, 1), :].rearrange("p a b -> p (a b)"), rows) \
                          .then_inc(x1_ready, 1)
                gate(dve, dve_passed, x1_ready, 2 * NA * (b + 1))
                nc.vector.bn_aggr(mv[:], bn[:].rearrange("p a b -> p (a b)")).then_inc(g_step, 1)
                dve.wait_ge(g_step, 3 * b + 1)
                nc.vector.tensor_copy(ex[:, 0:1], mv[:, 0:1]).then_inc(g_step, 1)
                nc.vector.scalar_tensor_tensor(out=ex[:, 1:2], in0=mv[:, 0:1], scalar=mv[:, 0:1], in1=mv[:, 1:2],
                                               op0=ALU.mult, op1=ALU.add).then_inc(g_step, 1)
                dve.wait_ge(g_sum, b + 1)
                group_scales(nc, dve, a_ps[:, 0:2], gst, gv, gn[:, 0:1], gn[:, 1:2], coef_step, b * (NORM + STEPS * GROUPS),
                             g_sq, 2 * b, g_root, b)

                with dve.Fori(0, GROUPS // 2) as i:
                    for par in range(2):
                        v = b * GROUPS + 2 * i + par
                        dve.wait_ge(v_done, v + 2)
                        dve.wait_ge(vrow_out[par], b * (8 * GROUPS) + 16 * i)
                        nc.vector.tensor_tensor(vrow[:, par], a_ps[:].rearrange("p (r c) -> p r c", c=C),
                                                bvalue_sb[:].unsqueeze(1).to_broadcast([P, COLS, C]),
                                                ALU.add).then_inc(vrow_ready, 1)

                def read_offsets(q, par):
                    n = b * GROUPS + q
                    dve.wait_ge(om_done, n + 1)
                    dve.wait_ge(corr_ready, n)
                    for half in range(2):
                        nc.vector.tensor_tensor(off[:, par, 2 * half:2 * half + 2, :],
                                                om_ps[:, half, 0:2 * OM].rearrange("p (r k) -> p r k", k=OM),
                                                bom_sb[:].unsqueeze(1).to_broadcast([P, 2, OM]),
                                                ALU.add).then_inc(off_ready, 1)

                def masks(q, par):
                    n = b * GROUPS + q
                    dve.wait_ge(dist_ready, 3 * n + 2)
                    nc.vector.tensor_scalar(near[:], dist[:, 1], 1.0, None, ALU.is_le).then_inc(near_step, 1)
                    dve.wait_ge(near_step, 3 * n + 1)
                    nc.vector.tensor_tensor(inside[:], near[:, :, 0:KG], near[:, :, KG:], ALU.mult) \
                      .then_inc(near_step, 1)
                    dve.wait_ge(near_step, 3 * n + 2)
                    nc.vector.tensor_tensor(mf[:, par], off[:, par, :, 2 * KG:], inside[:], ALU.mult) \
                      .then_inc(near_step, 1)
                    dve.wait_ge(cnt_done, n)
                    nc.vector.tensor_scalar(flag[:], inside[:], -1.0, 1.0, ALU.mult, ALU.add).then_inc(flag_ready, 1)

                def read_counts(q, par):
                    n = b * GROUPS + q
                    dve.wait_ge(cnt_done, n + 1)
                    c = cnt_ps[0:1, 0:COLS * KG]
                    nc.vector.tensor_copy(cnt[:, par], c).then_inc(cnt_ready, 1)
                    nc.vector.tensor_reduce(cntk[:, par], c.rearrange("p (k g) -> p k g", g=G), AX.X, ALU.add) \
                      .then_inc(cnt_ready, 1)
                    nc.vector.tensor_reduce(cntr[:, par], c.rearrange("p (r k) -> p r k", k=KG), AX.X, ALU.add) \
                      .then_inc(cnt_ready, 1)

                def weights(q, par):
                    n = b * GROUPS + q
                    s = b * (NORM + STEPS * GROUPS) + NORM + STEPS * q
                    dve.wait_ge(hat_ready, 3 * n + 3)
                    dve.wait_ge(near_step, 3 * n + 3)
                    nc.vector.memset(wt[:, par], 0.0).then_inc(coef_step, 1)
                    nc.vector.tensor_tensor(my[:], hat[:, :, :, KG:], mf[:, par].unsqueeze(1)
                                            .to_broadcast([P, 3, COLS, KG]), ALU.mult).then_inc(coef_step, 1)
                    dve.wait_ge(coef_step, s + 2)
                    for jx in range(3):
                        nc.vector.tensor_tensor(tt[:, jx], hat[:, jx, :, 0:KG].unsqueeze(1)
                                                .to_broadcast([P, 3, COLS, KG]), my[:], ALU.mult) \
                          .then_inc(coef_step, 1)
                    for i, (jx, jy) in enumerate((jx, jy) for jx in range(3) for jy in range(3)):
                        dve.wait_ge(coef_step, s + 5 + i)
                        acc = wt[:, par, :, jx:jx + KS, jy * G:(jy + KS) * G]
                        ins = nc.vector.tensor_tensor(
                            acc, acc, tt[:, jx, jy].rearrange("p r (a k) -> p r a k", a=KS), ALU.add)
                        ins.then_inc(coef_step if i < 8 else wt_ready, 1)

                def products(q, par, r):
                    slot = (COLS * par + r) % RING
                    if r == 0:
                        dve.wait_ge(wt_ready, b * GROUPS + q + 1)
                    dve.wait_ge(v_in[(r + 1) % 2], 16 * (b * LOADS[(r + 1) % 2] + 2 * q + (r + 3) // 2 + 1))
                    dve.wait_ge(v_in[r % 2], 16 * (b * LOADS[r % 2] + 2 * q + r // 2 + 3))
                    dve.wait_ge(sum_done, b * W + q * COLS + r)
                    for dx in range(TAPS):
                        ins = nc.vector.tensor_tensor(
                            prod[:, r % 2, dx].rearrange("p (t c) -> p t c", c=CG),
                            vring[:, (slot + dx) % RING].rearrange("p (t c) -> p t c", c=CG),
                            wt[:, par, r, dx].unsqueeze(2).to_broadcast([P, TAPS * G, CG]), ALU.mult)
                    ins.then_inc(prod_ready, 1)

                def sums(q, par):
                    n = b * GROUPS + q
                    dve.wait_ge(sum_done, COLS * (n + 1) + 1)
                    dve.wait_ge(corr_ready, n + 2)
                    dve.wait_ge(t_done, n)
                    nc.vector.tensor_tensor(ssum[:], sum_ps[:, par].rearrange("p (r c) -> p r c", c=C),
                                            corr[:, par], ALU.add).then_inc(ssum_ready, 1)

                def result(q):
                    n = b * GROUPS + q
                    dve.wait_ge(out_done, n + 1)
                    dst = cols[:, q * COLS:(q + 1) * COLS, :] if isinstance(q, int) else \
                        cols[:, bass.ds(q * COLS, COLS), :]
                    nc.vector.scalar_tensor_tensor(out=dst, in0=out_ps[:].rearrange("p (r y) -> p r y", y=H),
                                                   scalar=bout_sb[:, 0:1], in1=dst, op0=ALU.add,
                                                   op1=ALU.add).then_inc(res_ready, 1)

                def group(q, par, first=False, last=False):
                    products(q, par, 0)
                    if not first:
                        sums(q - 1, 1 - par)
                    if not last:
                        read_offsets(q + 1, 1 - par)
                    products(q, par, 1)
                    if not last:
                        masks(q + 1, 1 - par)
                    products(q, par, 2)
                    if not last:
                        read_counts(q + 1, 1 - par)
                        weights(q + 1, 1 - par)
                    products(q, par, 3)
                    if not first:
                        result(q - 1)

                read_offsets(0, 0)
                masks(0, 0)
                read_counts(0, 0)
                weights(0, 0)
                group(0, 0, first=True)
                with dve.Fori(0, (GROUPS - 2) // 2) as i:
                    group(2 * i + 1, 1)
                    group(2 * i + 2, 0)
                group(GROUPS - 1, 1, last=True)
                sums(GROUPS - 1, 1)
                result(GROUPS - 1)


def program(nc, x, w_qkv, b_qkv, bv, rel, w_proj, b_proj, w_value, b_value, w_om, b_om, w_out, b_out, out):
    attended = nc.dram_tensor("attended", (B, H, W, C), F32, kind="Internal").ap()
    rel_rows = nc.dram_tensor("rel_rows", (WS, NH * REL * WS), F32, kind="Internal").ap()
    parts_dram = nc.dram_tensor("parts_dram", (2, P, 3 * 2 * 2 * NT), BF16, kind="Internal").ap()
    vals = nc.dram_tensor("vals", (XP, YP, C), F32, kind="Internal").ap()
    attention(nc, x, w_qkv, b_qkv, bv, rel, attended, rel_rows, parts_dram)
    deformable(nc, x, attended, w_proj, b_proj, w_value, b_value, w_om, b_om, w_out, b_out, vals, out)


_OUT = ((B, C, H, W), "float32")


def kernel(x, L0_conv_qkv_w, L0_conv_qkv_b, L0_conv_proj_w, L0_conv_proj_b, L0_conv_bias_table,
           L1_conv_value_proj_w, L1_conv_value_proj_b, L1_conv_offset_mask_w, L1_conv_offset_mask_b,
           L1_conv_output_proj_w, L1_conv_output_proj_b):
    import numpy as np
    import concourse.bacc as bacc
    from concourse.bass_utils import run_bass_kernel_spmd

    def layout(a, *order):
        return np.ascontiguousarray(np.transpose(np.asarray(a), order) if order else np.asarray(a))

    g, ky, kx = np.meshgrid(np.arange(G), np.arange(KS), np.arange(KS), indexing="ij")
    point = ky * KS + kx
    rows = [g * 3 * K2 + 2 * point, g * 3 * K2 + 2 * point + 1, g * 3 * K2 + 2 * K2 + point]
    order = np.concatenate([np.transpose(r, (2, 1, 0)).reshape(-1) for r in rows])
    arrays = {
        "x": layout(x),
        "w_qkv": layout(L0_conv_qkv_w, 1, 0),
        "b_qkv": layout(np.asarray(L0_conv_qkv_b).reshape(3, C), 1, 0),
        "bv": layout(np.asarray(L0_conv_qkv_b)[2 * C:]),
        "rel": layout(np.asarray(L0_conv_bias_table).reshape(REL, REL, NH)[::-1, ::-1], 2, 0, 1).reshape(-1),
        "w_proj": layout(L0_conv_proj_w, 1, 0),
        "b_proj": layout(L0_conv_proj_b),
        "w_value": layout(L1_conv_value_proj_w, 1, 0),
        "b_value": layout(L1_conv_value_proj_b),
        "w_om": layout(np.asarray(L1_conv_offset_mask_w)[order], 1, 0),
        "b_om": layout(np.asarray(L1_conv_offset_mask_b)[order]),
        "w_out": layout(L1_conv_output_proj_w, 1, 0),
        "b_out": layout(np.asarray(L1_conv_output_proj_b).reshape(C, 1)),
    }
    nc = bacc.Bacc("TRN2", target_bir_lowering=False, num_devices=1)
    ins = {n: nc.dram_tensor(n, a.shape, F32, kind="ExternalInput").ap() for n, a in arrays.items()}
    out = nc.dram_tensor("out", _OUT[0], F32, kind="ExternalOutput").ap()
    program(nc, out=out, **ins)
    result = run_bass_kernel_spmd(nc, [arrays], core_ids=[0])
    return result.results[0]["out"]
```

```python
from contextlib import ExitStack

import concourse.bass as bass
from concourse import mybir

ALU = mybir.AluOpType
ACT = mybir.ActivationFunctionType
AX = mybir.AxisListType
F32 = mybir.dt.float32
BF16 = mybir.dt.bfloat16
I32 = mybir.dt.int32
U32 = mybir.dt.uint32

B, C, H, W = 2, 128, 128, 128
PIX = H * W
P = 128

WS = 16
NH = 8
HD = C // NH
NT = WS * WS
REL = 2 * WS - 1
PAIRS = B * (H // WS) * (W // WS) // 2
SLOTS = 2 * NH
TERMS = ((0, 0), (0, 1), (1, 0), (1, 1), (0, 2), (2, 0))
STACK = len(TERMS) * HD
VA = 32
SBIAS = 8
SCALE = float(HD) ** -0.5
T_LAG = 2
READ_LAG_A, READ_LAG_V = 3, 2
PV_LAG = 4
Q_AT, K_AT, V_AT = 0, 4, 8
OUT_AT = 6
AHEAD = 2
GN_EPS = 1e-5
CHUNK = 4 * W


KS = 3
K2 = KS * KS
G = 8
CG = C // G
OM = 3 * K2 * G
KG = K2 * G
TAPS = KS + 2
PAD = TAPS // 2
FAR_RING = 4
XP = W + 2 * PAD + 3
YP = H + 2 * PAD
COLS = 4
GROUPS = W // COLS
LAG = 3
RING = 8
AHEAD_V = RING - 1
INFO = 4 + COLS * G


def count(n):
    return max(n, 0) + 1 if isinstance(n, int) else n + 1


def start_counts(eng, sems):
    for s in sems:
        eng.sem_inc(s, 1)


def group_matrix(nc, pool, mat, ready):
    v = mat[:].rearrange("p (j i) -> p j i", i=4)
    nc.gpsimd.memset(mat[:], 0.25).then_inc(ready, 1)
    pool.wait_ge(ready, count(1))
    nc.gpsimd.affine_select(out=v, in_=v, compare_op=ALU.is_ge, fill=0.0, base=0,
                            pattern=[[-4, P // 4], [0, 4]], channel_multiplier=1).then_inc(ready, 1)
    pool.wait_ge(ready, count(2))
    nc.gpsimd.affine_select(out=v, in_=v, compare_op=ALU.is_ge, fill=0.0, base=3,
                            pattern=[[4, P // 4], [0, 4]], channel_multiplier=-1).then_inc(ready, 1)


def identity_matrix(nc, pool, mat, ready):
    nc.gpsimd.memset(mat[:], 0.0).then_inc(ready, 1)
    pool.wait_ge(ready, count(1))
    nc.gpsimd.affine_select(out=mat[:], in_=mat[:], compare_op=ALU.not_equal, fill=1.0, base=0,
                            pattern=[[-1, P]], channel_multiplier=1).then_inc(ready, 1)


def group_scales(nc, dve, moments, gst, gv, scale, shift, step, s0, part, p0, root, r0):
    nc.vector.tensor_copy(gst[:], moments).then_inc(step, 1)
    dve.wait_ge(step, count(s0 + 1))
    nc.vector.tensor_tensor(gv[:, 3:4], gst[:, 0:1], gst[:, 0:1], ALU.mult).then_inc(step, 1)
    dve.wait_ge(step, count(s0 + 2))
    nc.vector.tensor_tensor(gv[:, 2:3], gst[:, 1:2], gv[:, 3:4], ALU.subtract).then_inc(step, 1)
    dve.wait_ge(step, count(s0 + 3))
    nc.vector.tensor_scalar(gv[:, 0:1], gv[:, 2:3], GN_EPS, None, ALU.add).then_inc(part, 1)
    dve.wait_ge(root, count(r0 + 1))
    dve.wait_ge(part, count(p0 + 1))
    nc.vector.reciprocal(gv[:, 2:3], gv[:, 1:2]).then_inc(step, 1)
    dve.wait_ge(step, count(s0 + 4))
    nc.vector.tensor_tensor(gv[:, 3:4], gv[:, 2:3], gv[:, 2:3], ALU.mult).then_inc(step, 1)
    dve.wait_ge(step, count(s0 + 5))
    nc.vector.tensor_tensor(gv[:, 3:4], gv[:, 3:4], gv[:, 0:1], ALU.mult).then_inc(step, 1)
    dve.wait_ge(step, count(s0 + 6))
    nc.vector.tensor_scalar(gv[:, 3:4], gv[:, 3:4], -0.5, 1.5, ALU.mult, ALU.add).then_inc(step, 1)
    dve.wait_ge(step, count(s0 + 7))
    nc.vector.tensor_tensor(scale, gv[:, 2:3], gv[:, 3:4], ALU.mult).then_inc(step, 1)
    dve.wait_ge(step, count(s0 + 8))
    nc.vector.tensor_tensor(gv[:, 3:4], gst[:, 0:1], scale, ALU.mult).then_inc(step, 1)
    dve.wait_ge(step, count(s0 + 9))
    nc.vector.tensor_scalar(shift, gv[:, 3:4], -1.0, None, ALU.mult).then_inc(part, 1)


def sample_info(nc, pool, part, r, scratch, done):
    n = 0
    nc.gpsimd.memset(part, 0.0).then_inc(done, 1)
    for i, (pattern, base) in enumerate((([[1, KS], [0, KS], [0, G]], r - 1),
                                         ([[0, KS], [1, KS], [0, G]], -1),
                                         ([[0, KS], [0, KS], [1, G]], 0))):
        nc.gpsimd.iota(scratch[:, i, :], pattern=pattern, base=base, channel_multiplier=0).then_inc(done, 1)
    n += 4
    pool.wait_ge(done, count(INFO_STEPS * r + n))
    nc.gpsimd.tensor_copy(part[:, :, 0:3].rearrange("p j i -> p i j"), scratch[:]).then_inc(done, 1)
    nc.gpsimd.memset(part[:, :, 4 + r * G:4 + (r + 1) * G], 1.0).then_inc(done, 1)
    n += 2
    pool.wait_ge(done, count(INFO_STEPS * r + n))
    for g in range(G):
        v = part[:, :, 4 + r * G + g].rearrange("p (k g) -> p k g", g=G)
        nc.gpsimd.affine_select(out=v, in_=v, compare_op=ALU.is_equal, fill=0.0, base=-g,
                                pattern=[[0, K2], [1, G]], channel_multiplier=0).then_inc(done, 1)


INFO_STEPS = 6 + 8


def attention(nc, x, w_qkv, b_qkv, bv_row, rel_rev, attended, rel_rows, parts_dram, info_out):
    with ExitStack() as ctx:
        def sb(name, shape, dt=F32):
            return ctx.enter_context(nc.sbuf_tensor(name, shape, dt))

        counted = []

        def sem(name):
            counted.append(ctx.enter_context(nc.semaphore(name)))
            return counted[-1]

        wqkv_sb = sb("wqkv_sb", [P, 3 * C])
        bqkv_sb = sb("bqkv_sb", [P, 3])
        bqn_sb = sb("bqn_sb", [P, 1])
        bv_sb = sb("bv_sb", [P, C])
        ident = sb("a_ident", [P, P])
        gmat = sb("a_gmat", [P, P])
        nbias = sb("nbias", [P, NH, 2, NT])
        stats_in = sb("a_stats_in", [P, 2, 2048])
        bn = sb("a_bn", [P, PIX // 512, 6])
        mv = sb("a_mv", [P, 2])
        ex = sb("a_ex", [P, 2])
        gst = sb("a_gst", [P, 2])
        gv = sb("a_gv", [P, 4])
        gn = sb("a_gn", [P, B, 2])
        gnp = sb("a_gnp", [P, 2])
        strips = sb("strips", [P, 2 * WS * W])
        xraw = sb("xraw", [P, 2 * NT])
        xn = sb("xn", [P, 2, 2 * NT])
        qk = sb("qk", [P, 2, 2 * NT])
        rest = sb("rest", [P, 2, 2 * NT])
        parts = sb("parts", [P, 3, 2, 2 * NT], BF16)
        stack = sb("stack", [STACK, 2, 2, NH, 2 * NT], BF16)
        va = sb("va", [P, 2, 4, NH, VA])
        sbias = sb("sbias", [P, SBIAS, 2, NT])
        nmax = sb("nmax", [P, SBIAS, 2])
        prob = sb("prob", [P, 4, 2, NT])
        probT = sb("probT", [P, 8, 2, NT])
        oT = sb("oT", [P, 2, 2 * NT])
        rsum = sb("rsum", [P, 2 * NH])
        on = sb("on", [P, 4, 2, C])
        info_int = sb("info_int", [1, 3, KG], I32)
        info = [t[0:1].rearrange("p a b c -> p (a b c)")[:, 0:KG * INFO].rearrange("p (j i) -> p j i", i=INFO)
                for t in (sbias, probT)]

        s_ps = ctx.enter_context(nc.psum_tensor("s_ps", [P, 2, 2, NT], F32))
        pt_ps = ctx.enter_context(nc.psum_tensor("pt_ps", [P, 3, 2, NT], F32))
        o_ps = ctx.enter_context(nc.psum_tensor("o_ps", [P, 2 * NT], F32))
        x_ps = ctx.enter_context(nc.psum_tensor("x_ps", [P, 2 * NH * VA], F32))
        qkv_ps = ctx.enter_context(nc.psum_tensor("qkv_ps", [P, 512], F32))
        x_view = x_ps[:].rearrange("p (a h c) -> p a h c", a=2, h=NH)

        weights_in = sem("weights_in")
        info_step = sem("info_step")
        info_stored = sem("info_stored")
        rows_out = sem("rows_out")
        bias_in = sem("bias_in")
        bias_neg = sem("bias_neg")
        bq_neg = sem("bq_neg")
        va_ones = sem("va_ones")
        id_ready = sem("id_ready")
        gmat_ready = sem("gmat_ready")
        st_in = [sem("st_in0"), sem("st_in1")]
        st_used = sem("st_used")
        gn_step = sem("gn_step")
        gn_sum = sem("gn_sum")
        gn_root = sem("gn_root")
        gn_ready = sem("gn_ready")
        chunk_in = [sem("chunk_in0"), sem("chunk_in1")]
        win_copied = sem("win_copied")
        gnp_ready = sem("gnp_ready")
        xn_ready = sem("xn_ready")
        q_done = sem("q_done")
        k_done = sem("k_done")
        v_done = sem("v_done")
        q_read = sem("q_read")
        k_read = sem("k_read")
        v_read = sem("v_read")
        split_step = sem("split_step")
        parts_out = sem("parts_out")
        stack_in = sem("stack_in")
        s_done = sem("s_done")
        max_done = sem("max_done")
        exp_done = sem("exp_done")
        t_done = sem("t_done")
        t_read_v = sem("t_read_v")
        t_read_a = sem("t_read_a")
        pv_done = sem("pv_done")
        recip_done = sem("recip_done")
        o_read = sem("o_read")
        x_done = sem("x_done")
        norm_done = sem("norm_done")
        y_out = [sem("y_out0"), sem("y_out1")]
        sp_passed = sem("sp_passed")
        pool_passed = sem("pool_passed")
        dve_passed = sem("dve_passed")

        block = ctx.enter_context(nc.Block())

        T_BANK = (0, 1, 2, 1)
        NSTAT = PIX // 2048
        x_chan = x.rearrange("b c h w -> b c (h w)")

        def token_rows(dram, p, w, half):
            strip = p // 4
            at = strip * (WS * W * C) + half * (NT // 2 // WS * W * C) + ((p % 4) * 2 + w) * (WS * C)
            return bass.AP(dram.tensor, dram.offset + at, [[W * C, NT // 2 // WS], [C, WS], [1, C]])

        @block.sync
        def _(sp):
            start_counts(sp, counted)
            for t, src in ((wqkv_sb, w_qkv), (bqkv_sb, b_qkv)):
                sp.dma_start(t[:], src).then_inc(weights_in, 16)
            sp.dma_start(bv_sb[:], bv_row.partition_broadcast(P)).then_inc(weights_in, 16)
            for xq in range(WS):
                src = bass.AP(rel_rev.tensor, rel_rev.offset + WS - 1 - xq, [[REL, NH * REL], [1, WS]])
                dst = rel_rows[xq].rearrange("(r k) -> r k", k=WS)
                sp.dma_start(dst, src).then_inc(rows_out, 16)
            for b in range(B):
                for n in range(NSTAT):
                    i = b * NSTAT + n
                    if i >= 2:
                        sp.wait_ge(st_used, count(i - 1))
                    sp.dma_start(stats_in[:, i % 2, :], x_chan[b][:, n * 2048:(n + 1) * 2048]) \
                      .then_inc(st_in[i % 2], 16)
            sp.wait_ge(rows_out, count(16 * WS))
            for yq in range(WS):
                half, row = yq // 8, yq % 8
                src = bass.AP(rel_rows.tensor, rel_rows.offset + (WS - 1 - yq) * WS,
                              [[NH * REL * WS, WS], [REL * WS, NH], [1, NT]])
                sp.dma_start(nbias[row * WS:(row + 1) * WS, :, half, :], src).then_inc(bias_in, 16)
            for n in range(6):
                if n >= 2:
                    sp.wait_ge(chunk_in[n % 2], count(16 * (n // 2)))
                sp.dma_start(strips[:, n * CHUNK:(n + 1) * CHUNK],
                             x_chan[0][:, n * CHUNK:(n + 1) * CHUNK]).then_inc(chunk_in[n % 2], 16)
            for r in range(COLS):
                sp.wait_ge(info_step, count(INFO_STEPS * (r + 1)))
                sp.wait_ge(info_stored, count(16 * r))
                sp.dma_start(info_out[r * KG:(r + 1) * KG].rearrange("j i -> (j i)").unsqueeze(0),
                             info[r % 2].rearrange("p j i -> p (j i)")).then_inc(info_stored, 16)
            sp.wait_ge(info_stored, count(16 * COLS))

            def store_parts(p, par):
                sp.wait_ge(split_step, count(4 * p + 4))
                sp.sem_inc(sp_passed, 1)
                sp.wait_ge(stack_in, count(16 * 2 * len(TERMS) * (p - 1)))
                sp.dma_start(parts_dram[par], parts[:].rearrange("p a b n -> p (a b n)")).then_inc(parts_out, 16)

            def restack(p, par):
                sp.wait_ge(parts_out, count(16 * p + 16))
                sp.sem_inc(sp_passed, 1)
                sp.wait_ge(s_done, count(SLOTS * (p - 1)))
                for t, (tq, tk) in enumerate(TERMS):
                    for qk_i, part in ((0, tq), (1, tk)):
                        row = 3 * 2 * 2 * NT
                        src = bass.AP(parts_dram.tensor,
                                      parts_dram.offset + par * P * row + (part * 2 + qk_i) * 2 * NT,
                                      [[row, HD], [HD * row, NH], [1, 2 * NT]])
                        sp.dma_start(stack[t * HD:(t + 1) * HD, par, qk_i], src).then_inc(stack_in, 16)

            def store(p, w, par):
                sp.wait_ge(norm_done, count(2 * (2 * p + w) + 2))
                for half in range(2):
                    sp.dma_start(token_rows(attended, p, w, half), on[:, 2 * par + w, half, :]) \
                      .then_inc(y_out[par], 16)

            def pair(p, par, first=False, left=AHEAD):
                if left == AHEAD:
                    sp.wait_ge(win_copied, count(p + 2))
                    sp.wait_ge(chunk_in[par], count(16 * (p // 2 + 3)))
                    q = (p + 6) % PAIRS
                    sp.dma_start(strips[:, bass.ds(((p + 6) % 8) * CHUNK, CHUNK)],
                                 bass.AP(x.tensor, x.offset + (q // 32) * (C * PIX) + (q % 32) * CHUNK,
                                         [[PIX, P], [1, CHUNK]])).then_inc(chunk_in[par], 16)
                if left >= 1:
                    restack(p + 1, 1 - par)
                if not first:
                    store(p - 1, 1, 1 - par)
                if left == AHEAD:
                    store_parts(p + 2, par)
                store(p, 0, par)

            store_parts(0, 0)
            restack(0, 0)
            store_parts(1, 1)
            pair(0, 0, first=True)
            with sp.Fori(0, (PAIRS - 4) // 2) as i:
                pair(2 * i + 1, 1)
                pair(2 * i + 2, 0)
            pair(PAIRS - 3, 1)
            pair(PAIRS - 2, 0, left=1)
            pair(PAIRS - 1, 1, left=0)
            store(PAIRS - 1, 1, 1)
            for par in range(2):
                sp.wait_ge(y_out[par], count(64 * (PAIRS // 2)))

        @block.gpsimd
        def _(pool):
            identity_matrix(nc, pool, ident, id_ready)
            group_matrix(nc, pool, gmat, gmat_ready)
            nc.gpsimd.memset(va[:], 0.0).then_inc(va_ones, 1)
            pool.wait_ge(va_ones, count(1))
            nc.gpsimd.memset(va[:, :, :, :, HD:HD + 1], 1.0).then_inc(va_ones, 1)
            for r in range(COLS):
                if r >= 2:
                    pool.wait_ge(info_stored, count(16 * (r - 1)))
                sample_info(nc, pool, info[r % 2], r, info_int, info_step)

            def normalise(p, par):
                pool.wait_ge(chunk_in[par], count(16 * (p // 2 + 2)))
                pool.wait_ge(chunk_in[1 - par], count(16 * (p // 2 + 2 + par)))
                src = strips[:, bass.ds(((p // 4) % 2) * (WS * W) + (p % 4) * 2 * WS, (WS - 1) * W + 2 * WS)]
                src = bass.AP(src.tensor, src.offset, [src.ap[0], [W, WS], [WS, 2], [1, WS]])
                dst = xraw[:].rearrange("p (w r c) -> p r w c", w=2, r=WS)
                pool.wait_ge(xn_ready, count(p))
                pool.sem_inc(pool_passed, 1)
                nc.gpsimd.tensor_copy(dst, src).then_inc(win_copied, 1)
                nc.gpsimd.tensor_copy(gnp[:], gn[:, bass.ds(p // 32, 1), :]).then_inc(gnp_ready, 1)
                pool.wait_ge(win_copied, count(p + 1))
                pool.sem_inc(pool_passed, 1)
                pool.wait_ge(gnp_ready, count(p + 1))
                pool.sem_inc(pool_passed, 1)
                pool.wait_ge(v_done, count(p - 1))
                pool.sem_inc(pool_passed, 1)
                nc.gpsimd.tensor_scalar(xn[:, par, :], xraw[:], gnp[:, 0:1], gnp[:, 1:2],
                                        ALU.mult, ALU.add).then_inc(xn_ready, 1)

            def split(p):
                pool.wait_ge(q_read, count(p + 1))
                pool.wait_ge(k_read, count(p + 1))
                pool.wait_ge(parts_out, count(16 * p))
                pool.sem_inc(pool_passed, 1)
                nc.gpsimd.tensor_copy(parts[:, 0], qk[:]).then_inc(split_step, 1)
                pool.wait_ge(split_step, count(4 * p + 1))
                pool.sem_inc(pool_passed, 1)
                nc.gpsimd.tensor_tensor(rest[:], qk[:], parts[:, 0], ALU.subtract).then_inc(split_step, 1)
                pool.wait_ge(split_step, count(4 * p + 2))
                pool.sem_inc(pool_passed, 1)
                nc.gpsimd.tensor_copy(parts[:, 1], rest[:]).then_inc(split_step, 1)
                pool.wait_ge(split_step, count(4 * p + 3))
                pool.sem_inc(pool_passed, 1)
                nc.gpsimd.tensor_tensor(parts[:, 2], rest[:], parts[:, 1], ALU.subtract).then_inc(split_step, 1)

            pool.wait_ge(gn_ready, count(2 * B))
            normalise(0, 0)
            split(0)
            normalise(1, 1)
            split(1)
            with pool.Fori(0, (PAIRS - 2) // 2) as i:
                for par in range(2):
                    normalise(2 * i + 2 + par, par)
                    split(2 * i + 2 + par)

        @block.tensor
        def _(pe):
            pe.wait_ge(weights_in, count(48))
            pe.wait_ge(id_ready, count(2))
            pe.wait_ge(gmat_ready, count(3))
            for b in range(B):
                pe.wait_ge(gn_step, count(3 * b + 3))
                nc.tensor.matmul(x_ps[:, 0:2], gmat[:], ex[:], start=True, stop=True).then_inc(gn_sum, 1)

            def proj_q(p, par):
                pe.wait_ge(xn_ready, count(p + 1))
                pe.wait_ge(k_read, count(p))
                pe.wait_ge(v_read, count(p - 1))
                nc.tensor.matmul(qkv_ps[:], wqkv_sb[:, 0:C], xn[:, par, :], start=True, stop=True).then_inc(q_done, 1)

            def proj_k(p, par):
                pe.wait_ge(q_read, count(p + 1))
                nc.tensor.matmul(qkv_ps[:], wqkv_sb[:, C:2 * C], xn[:, par, :], start=True, stop=True) \
                  .then_inc(k_done, 1)

            def proj_v(p, par):
                pe.wait_ge(k_read, count(min(p + 2, PAIRS) if isinstance(p, int) else p + 2))
                for n in range(4):
                    mm = nc.tensor.matmul(qkv_ps[:, n * C:(n + 1) * C], xn[:, par, n * P:(n + 1) * P],
                                          wqkv_sb[:, 2 * C:3 * C], start=True, stop=True)
                mm.then_inc(v_done, 1)

            def scores(p, n, par):
                w, h = divmod(n, NH)
                if n == 0:
                    pe.wait_ge(stack_in, count(16 * 2 * len(TERMS) * (p + 1)))
                g = SLOTS * p + n
                pe.wait_ge(max_done, count(g - 1))
                for half in range(2):
                    at = w * NT + half * P
                    mm = nc.tensor.matmul(s_ps[:, n % 2, half, :], stack[:, par, 0, h, at:at + P],
                                          stack[:, par, 1, h, w * NT:(w + 1) * NT], start=True, stop=True)
                mm.then_inc(s_done, 1)

            def turn(p, n):
                g = SLOTS * p + n
                pe.wait_ge(exp_done, count(g + 1))
                if n % 2 == 0:
                    pe.wait_ge(t_read_a, count(NH * p + n // 2 - 1))
                else:
                    pe.wait_ge(t_read_v, count(NH * p + n // 2))
                for half in range(2):
                    for kh in range(2):
                        mm = nc.tensor.transpose(pt_ps[:, T_BANK[n % 4], kh, half * P:(half + 1) * P],
                                                 prob[:, n % 4, half, kh * P:(kh + 1) * P], ident[:])
                mm.then_inc(t_done, 1)

            def weigh(p, k, par):
                w, t = divmod(k, 2)
                pe.wait_ge(t_read_a, count(NH * p + 2 * k + 2))
                pe.wait_ge(t_read_v, count(NH * p + 2 * k + 2))
                if k == 0:
                    pe.wait_ge(v_read, count(p + 1))
                if t == 0:
                    pe.wait_ge(o_read, count(2 * p + w))
                for kh in range(2):
                    for j in range(4):
                        mm = nc.tensor.matmul(o_ps[32 * j:32 * j + VA, t * NT:(t + 1) * NT],
                                              va[:, par, 2 * w + kh, 4 * t + j, :],
                                              probT[:, (4 * k + j) % 8, kh, :], start=(kh == 0), stop=(kh == 1))
                mm.then_inc(pv_done, 1)

            def turn_out(win, w):
                pe.wait_ge(o_read, count(win + 1))
                pe.wait_ge(norm_done, count(2 * win))
                for half in range(2):
                    for t in range(2):
                        at = (2 * half + t) * P
                        mm = nc.tensor.transpose(x_ps[:, at:at + P], oT[:, w, t * NT + half * P:t * NT + (half + 1) * P],
                                                 ident[:])
                mm.then_inc(x_done, 1)

            def pair(p, par, first=False, left=AHEAD):
                for n in range(SLOTS):
                    scores(p, n, par)
                    if n >= T_LAG:
                        turn(p, n - T_LAG)
                    elif not first:
                        turn(p - 1, n - T_LAG + SLOTS)
                    if n % 4 == 3:
                        if n > 3:
                            weigh(p, (n - 7) // 4, par)
                        elif not first:
                            weigh(p - 1, 3, 1 - par)
                    if n == OUT_AT and not first:
                        turn_out(2 * p - 1, 1)
                    if n == NH + OUT_AT:
                        turn_out(2 * p, 0)
                    if n == Q_AT and left == AHEAD:
                        proj_q(p + 2, par)
                    if n == K_AT and left == AHEAD:
                        proj_k(p + 2, par)
                    if n == V_AT and left >= 1:
                        proj_v(p + 1, 1 - par)

            proj_q(0, 0)
            proj_k(0, 0)
            proj_q(1, 1)
            proj_k(1, 1)
            proj_v(0, 0)
            pair(0, 0, first=True)
            with pe.Fori(0, (PAIRS - 4) // 2) as i:
                pair(2 * i + 1, 1)
                pair(2 * i + 2, 0)
            pair(PAIRS - 3, 1)
            pair(PAIRS - 2, 0, left=1)
            pair(PAIRS - 1, 1, left=0)
            for n in range(SLOTS - T_LAG, SLOTS):
                turn(PAIRS - 1, n)
            weigh(PAIRS - 1, 3, 1)
            turn_out(2 * PAIRS - 1, 1)

        @block.scalar
        def _(act):
            for b in range(B):
                act.wait_ge(gn_ready, count(2 * b + 1))
                nc.scalar.activation(gv[:, 1:2], gv[:, 0:1], ACT.Sqrt).then_inc(gn_root, 1)
            act.wait_ge(weights_in, count(48))
            nc.scalar.mul(bqn_sb[:], bqkv_sb[:, 0:1], -SCALE).then_inc(bq_neg, 1)
            act.wait_ge(bq_neg, count(1))

            def read_q(p):
                act.wait_ge(q_done, count(p + 1))
                act.wait_ge(split_step, count(4 * p))
                nc.scalar.activation(qk[:, 0, :], qkv_ps[:], ACT.Identity, bias=bqn_sb[:, 0:1],
                                     scale=-SCALE).then_inc(q_read, 1)

            def read_k(p):
                act.wait_ge(k_done, count(p + 1))
                nc.scalar.activation(qk[:, 1, :], qkv_ps[:], ACT.Identity, bias=bqkv_sb[:, 1:2]).then_inc(k_read, 1)

            def exp(p, n):
                g = SLOTS * p + n
                act.wait_ge(max_done, count(g + 1))
                act.wait_ge(t_done, count(g - 3))
                for half in range(2):
                    ins = nc.scalar.activation(prob[:, n % 4, half, :], sbias[:, n % SBIAS, half, :], ACT.Exp,
                                               bias=nmax[:, n % SBIAS, half:half + 1], scale=-1.0)
                ins.then_inc(exp_done, 1)

            def read_turned(p, n):
                act.wait_ge(t_done, count(SLOTS * p + n + 1))
                act.wait_ge(pv_done, count(4 * p + n // 4 - 1))
                nc.scalar.copy(probT[:, n % 8], pt_ps[:, T_BANK[n % 4]]).then_inc(t_read_a, 1)

            def read_o(win, w):
                act.wait_ge(pv_done, count(2 * (win + 1)))
                act.wait_ge(x_done, count(win - 1))
                nc.scalar.copy(oT[:, w], o_ps[:]).then_inc(o_read, 1)

            def pair(p, first=False, left=AHEAD):
                for n in range(SLOTS):
                    exp(p, n)
                    m = n - READ_LAG_A
                    if m % 2 == 0 and not (first and m < 0):
                        read_turned(p if m >= 0 else p - 1, m % SLOTS)
                    if n == PV_LAG and not first:
                        read_o(2 * p - 1, 1)
                    if n == NH + PV_LAG:
                        read_o(2 * p, 0)
                    if n == Q_AT + 1 and left == AHEAD:
                        read_q(p + 2)
                    if n == K_AT and left == AHEAD:
                        read_k(p + 2)

            for p in range(AHEAD):
                read_q(p)
                read_k(p)
            pair(0, first=True)
            with act.Fori(0, (PAIRS - 4) // 2) as i:
                pair(2 * i + 1)
                pair(2 * i + 2)
            pair(PAIRS - 3)
            pair(PAIRS - 2, left=1)
            pair(PAIRS - 1, left=0)
            for m in range(SLOTS - READ_LAG_A, SLOTS):
                if m % 2 == 0:
                    read_turned(PAIRS - 1, m)
            read_o(2 * PAIRS - 1, 1)

        @block.vector
        def _(dve):
            for b in range(B):
                for n in range(NSTAT):
                    i = b * NSTAT + n
                    dve.wait_ge(st_in[i % 2], count(16 * (i // 2 + 1)))
                    for m in range(4):
                        ins = nc.vector.bn_stats(bn[:, 4 * n + m, :], stats_in[:, i % 2, m * 512:(m + 1) * 512])
                    ins.then_inc(st_used, 1)
                dve.wait_ge(st_used, count(NSTAT * (b + 1)))
                nc.vector.bn_aggr(mv[:], bn[:].rearrange("p a b -> p (a b)")).then_inc(gn_step, 1)
                dve.wait_ge(gn_step, count(3 * b + 1))
                nc.vector.tensor_copy(ex[:, 0:1], mv[:, 0:1]).then_inc(gn_step, 1)
                nc.vector.scalar_tensor_tensor(out=ex[:, 1:2], in0=mv[:, 0:1], scalar=mv[:, 0:1], in1=mv[:, 1:2],
                                               op0=ALU.mult, op1=ALU.add).then_inc(gn_step, 1)
                dve.wait_ge(gn_sum, count(b + 1))
                group_scales(nc, dve, x_ps[:, 0:2], gst, gv, gn[:, b, 0:1], gn[:, b, 1:2], recip_done, 9 * b,
                             gn_ready, 2 * b, gn_root, b)
            RB = 9 * B
            dve.wait_ge(bias_in, count(16 * WS))
            nc.vector.tensor_scalar(nbias[:].rearrange("p h a k -> p (h a k)"),
                                    nbias[:].rearrange("p h a k -> p (h a k)"), -1.0, None,
                                    ALU.mult).then_inc(bias_neg, 1)
            dve.wait_ge(bias_neg, count(1))
            dve.wait_ge(va_ones, count(2))
            dve.wait_ge(weights_in, count(48))

            def read_v(p, par):
                dve.wait_ge(v_done, count(p + 1))
                dve.wait_ge(pv_done, count(4 * (p - 1)))
                nc.vector.tensor_tensor(va[:, par, :, :, 0:HD],
                                        qkv_ps[:].rearrange("p (n h c) -> p n h c", n=4, h=NH),
                                        bv_sb[:].rearrange("p (h c) -> p h c", h=NH).unsqueeze(1)
                                        .to_broadcast([P, 4, NH, HD]),
                                        ALU.add).then_inc(v_read, 1)

            def bias_max(p, n):
                g = SLOTS * p + n
                h = n % NH
                dve.wait_ge(s_done, count(g + 1))
                dve.sem_inc(dve_passed, 1)
                for half in range(2):
                    ins = nc.vector.tensor_tensor_reduce(
                        out=sbias[:, n % SBIAS, half, :], in0=s_ps[:, n % 2, half, :], in1=nbias[:, h, half, :],
                        scale=1.0, scalar=3.0e38, op0=ALU.add, op1=ALU.min,
                        accum_out=nmax[:, n % SBIAS, half:half + 1])
                ins.then_inc(max_done, 1)

            def read_turned(p, n):
                dve.wait_ge(t_done, count(SLOTS * p + n + 1))
                dve.wait_ge(pv_done, count(4 * p + n // 4 - 1))
                nc.vector.tensor_copy(probT[:, n % 8], pt_ps[:, T_BANK[n % 4]]).then_inc(t_read_v, 1)

            def norm(win, w, par, k):
                dve.wait_ge(x_done, count(win + 1))
                dve.wait_ge(norm_done, count(2 * win))
                nc.vector.reciprocal(rsum[:].rearrange("p (a h) -> p a h", h=NH),
                                     x_view[:, :, :, HD]).then_inc(recip_done, 1)
                dve.wait_ge(recip_done, count(RB + win + 1))
                dve.wait_ge(y_out[par], count(64 * k))
                for half in range(2):
                    nc.vector.tensor_tensor(on[:, 2 * par + w, half, :].rearrange("p (h c) -> p h c", h=NH),
                                            x_view[:, half, :, 0:HD],
                                            rsum[:, half * NH:(half + 1) * NH].unsqueeze(2)
                                            .to_broadcast([P, NH, HD]), ALU.mult).then_inc(norm_done, 1)

            def pair(p, par, first=False, left=AHEAD):
                for n in range(SLOTS):
                    bias_max(p, n)
                    m = n - READ_LAG_V
                    if m % 2 == 1 and not (first and m < 0):
                        read_turned(p if m >= 0 else p - 1, m % SLOTS)
                    if n == OUT_AT + 1 and not first:
                        norm(2 * p - 1, 1, 1 - par, (p - 1) // 2)
                    if n == NH + OUT_AT + 1:
                        norm(2 * p, 0, par, p // 2)
                    if n == V_AT + 1 and left >= 1:
                        read_v(p + 1, 1 - par)

            read_v(0, 0)
            pair(0, 0, first=True)
            with dve.Fori(0, (PAIRS - 4) // 2) as i:
                pair(2 * i + 1, 1)
                pair(2 * i + 2, 0)
            pair(PAIRS - 3, 1)
            pair(PAIRS - 2, 0, left=1)
            pair(PAIRS - 1, 1, left=0)
            for m in range(SLOTS - READ_LAG_V, SLOTS):
                if m % 2 == 1:
                    read_turned(PAIRS - 1, m)
            norm(2 * PAIRS - 1, 1, 1, (PAIRS - 1) // 2)


def deformable(nc, x, attended, w_proj, bproj_row, w_value, bv_row, w_om, bom_row, w_out, b_out,
               vals, off_out, info_out, out):
    with ExitStack() as ctx:
        def sb(name, shape, dt=F32):
            return ctx.enter_context(nc.sbuf_tensor(name, shape, dt))

        counted = []

        def sem(name):
            counted.append(ctx.enter_context(nc.semaphore(name)))
            return counted[-1]

        wproj_sb = sb("wproj_sb", [P, C])
        bproj_sb = sb("bproj_sb", [P, W])
        wvalue_sb = sb("wvalue_sb", [P, C])
        bvalue_sb = sb("bvalue_sb", [P, C])
        wom_sb = sb("wom_sb", [P, OM])
        bom_sb = sb("bom_sb", [P, OM])
        wout_sb = sb("wout_sb", [P, C])
        bout_sb = sb("bout_sb", [P, 1])
        ident = sb("d_ident", [P, P])
        gmat = sb("d_gmat", [P, P])
        ones = sb("ones", [P, 1], BF16)
        one_col = sb("one_col", [P, 3])
        x1 = sb("x1", [P, PIX])
        bn = sb("d_bn", [P, PIX // 512, 6])
        mv = sb("d_mv", [P, 2])
        ex = sb("d_ex", [P, 2])
        gst = sb("d_gst", [P, 2])
        gv = sb("d_gv", [P, 4])
        gn = sb("d_gn", [P, 2])
        xn = sb("d_xn", [P, 2, COLS, H])
        vring = sb("vring", [P, RING, TAPS * C])
        att = vring[:, 0:2, 0:COLS * C].rearrange("p s (r c) -> p s r c", c=C)
        vrow = vring[:, 2:4, 0:COLS * C].rearrange("p s (r c) -> p s r c", c=C)
        off = sb("off", [P, FAR_RING, COLS, KG, 3])
        dist = sb("dist", [P, 3, COLS, 2 * KG])
        hat = sb("hat", [P, 3, COLS, 2 * KG])
        reach = sb("reach", [P, COLS, KG])
        keytab = sb("keytab", [P, COLS * KG])
        keys = sb("keys", [P, FAR_RING, COLS * KG])
        top = sb("top", [P, 8])
        flag = sb("flag", [P, 8], BF16)
        far = sb("far", [P, FAR_RING, 8])
        at8 = sb("at8", [P, 8])
        far_at = sb("far_at", [P, FAR_RING, 2, 8], I32)
        least = sb("least", [P, FAR_RING])
        some = sb("some", [1, 8])
        total = sb("total", [1, 1])
        rounds = sb("rounds", [1, FAR_RING], I32)
        mf = sb("mf", [P, 2, COLS, KG])
        my = sb("my", [P, 3, COLS, KG])
        tt = sb("tt", [P, 3, 3, COLS, KG])
        wt = sb("wt", [P, 2, COLS, TAPS, TAPS * G])
        prod = sb("prod", [P, 2, TAPS, TAPS * C])
        zeros = prod[:, 0].rearrange("p t c -> p (t c)")[:, 0:YP * C // 16]
        ssum = sb("ssum", [P, FAR_RING, COLS, C])
        sT = sb("sT", [P, COLS * H])
        scratch = sb("scratch", [P, COLS * KG], I32)
        row_at = sb("row_at", [P, 1])
        first_at = sb("first_at", [P, GROUPS, 2])
        pos = sb("pos", [P, 2], I32)
        is_far = sb("is_far", [P, 1])
        o_sel = sb("o_sel", [P, 3])
        i_sel = sb("i_sel", [P, INFO])
        loc = sb("loc", [P, 2])
        loci = sb("loci", [P, 2], I32)
        low = sb("low", [P, 2])
        gap = sb("gap", [P, 2])
        side = sb("side", [P, 2, 2])
        wm = sb("wm", [P, 1])
        wy = sb("wy", [P, 2])
        w4 = sb("w4", [P, 2, 2])
        idxf = sb("idxf", [P, 1])
        idx = sb("idx", [P, 1], I32)
        gath = sb("gath", [P, 2, 2, CG])
        gval = sb("gval", [P, CG])
        spread = sb("spread", [P, COLS, G, CG])
        rest = sb("d_rest", [P, COLS * KG])
        key_sum = sb("key_sum", [1, COLS * KG])
        key_left = sb("key_left", [1, COLS * KG], I32)
        KI = COLS * KG

        om_ps = ctx.enter_context(nc.psum_tensor("om_ps", [P, 2, 512], F32))
        sum_ps = ctx.enter_context(nc.psum_tensor("sum_ps", [P, 2, COLS * C], F32))
        t_ps = ctx.enter_context(nc.psum_tensor("t_ps", [P, COLS * H], F32))
        out_ps = ctx.enter_context(nc.psum_tensor("out_ps", [P, COLS * H], F32))
        cnt_ps = ctx.enter_context(nc.psum_tensor("cnt_ps", [P, 512], F32))
        a_ps = ctx.enter_context(nc.psum_tensor("a_ps", [P, 512], F32))

        w_in = sem("w_in")
        pad_out = sem("pad_out")
        consts = sem("consts")
        ones_ready = sem("ones_ready")
        zeros_ready = sem("zeros_ready")
        d_id = sem("d_id")
        d_gm = sem("d_gm")
        x_in = sem("x_in")
        att_in = [sem("att_in0"), sem("att_in1")]
        a_done = sem("a_done")
        a_read = sem("a_read")
        b_added = sem("b_added")
        x1_ready = sem("x1_ready")
        g_step = sem("g_step")
        g_sum = sem("g_sum")
        g_root = sem("g_root")
        g_sq = sem("g_sq")
        vn_ready = sem("vn_ready")
        v_done = sem("dv_done")
        vrow_ready = sem("vrow_ready")
        vrow_out = [sem("vrow_out0"), sem("vrow_out1")]
        v_in = [sem("v_in0"), sem("v_in1")]
        xn_ready = sem("dxn_ready")
        om_done = sem("om_done")
        off_ready = sem("off_ready")
        dist_ready = sem("dist_ready")
        hat_ready = sem("hat_ready")
        near_step = sem("near_step")
        top_ready = sem("top_ready")
        flag_ready = sem("flag_ready")
        key_ready = sem("key_ready")
        cnt_done = sem("cnt_done")
        cnt_step = sem("cnt_step")
        cnt_ready = sem("cnt_ready")
        coef_step = sem("coef_step")
        wt_zero = sem("wt_zero")
        wt_ready = sem("wt_ready")
        prod_ready = sem("prod_ready")
        sum_done = sem("sum_done")
        far_done = sem("far_done")
        ssum_ready = sem("ssum_ready")
        t_done = sem("dt_done")
        sT_ready = sem("sT_ready")
        out_done = sem("out_done")
        res_ready = sem("res_ready")
        stored = sem("stored")
        sp_passed = sem("d_sp_passed")
        pool_passed = sem("d_pool_passed")
        dve_passed = sem("d_dve_passed")
        far_step = ctx.enter_context(nc.semaphore("far_step"))
        gathered = ctx.enter_context(nc.semaphore("gathered"))
        fetched = ctx.enter_context(nc.semaphore("fetched"))
        off_stored = sem("off_stored")

        block = ctx.enter_context(nc.Block())

        x_chan = x.rearrange("b c h w -> b c (h w)")
        out_chan = out.rearrange("b c h w -> b c (h w)")
        QUARTER = PIX // 4
        cols = x1[:].rearrange("p (y x) -> p x y", x=W)
        LOOPS = (GROUPS - LAG - 2) // FAR_RING
        NA = H // COLS
        LOADS = ((W + AHEAD_V + 1) // 2, (W + AHEAD_V) // 2)

        def at(dram, offset, dims):
            return bass.AP(dram.tensor, dram.offset + offset, dims)

        @block.sync
        def _(sp):
            start_counts(sp, counted)
            for t, src in ((wproj_sb, w_proj), (wvalue_sb, w_value), (wom_sb, w_om), (wout_sb, w_out),
                           (bout_sb, b_out)):
                sp.dma_start(t[:], src).then_inc(w_in, 16)
            for t, src in ((bproj_sb, bproj_row), (bvalue_sb, bv_row), (bom_sb, bom_row)):
                sp.dma_start(t[:], src.partition_broadcast(P)).then_inc(w_in, 16)
            sp.wait_ge(zeros_ready, count(1))
            for col in (*range(PAD), *range(PAD + W, XP)):
                sp.dma_start(at(vals, col * YP * C, [[YP * C // 16, 16], [1, YP * C // 16]]),
                             zeros[0:16, :]).then_inc(pad_out, 16)
            for row in (0, PAD + H):
                sp.dma_start(at(vals, (PAD * YP + row) * C, [[YP * C, W], [1, PAD * C]]),
                             zeros[:, 0:PAD * C]).then_inc(pad_out, 16)
            NPAD = XP - W + 2
            sp.wait_ge(pad_out, count(16 * NPAD))

            with sp.Fori(0, B) as b:
                sp.wait_ge(stored, count(64 * b))
                for n in range(4):
                    sp.dma_start(x1[:, n * QUARTER:(n + 1) * QUARTER],
                                 at(x, b * (C * PIX) + n * QUARTER, [[PIX, P], [1, QUARTER]])).then_inc(x_in, 16)
                with sp.Fori(0, NA // 2) as i:
                    for par in range(2):
                        a = b * NA + 2 * i + par
                        sp.wait_ge(a_done, count(a))
                        sp.sem_inc(sp_passed, 1)
                        sp.wait_ge(att_in[par], count(8 * (a - par)))
                        sp.sem_inc(sp_passed, 1)
                        sp.dma_start(att[:, par], at(attended, a * (COLS * W * C), [[C, P], [W * C, COLS], [1, C]])) \
                          .then_inc(att_in[par], 16)
                with sp.Fori(0, GROUPS // 2) as i:
                    for par in range(2):
                        v = b * GROUPS + 2 * i + par
                        sp.wait_ge(vrow_ready, count(v + 2))
                        sp.dma_start(at(vals, ((PAD + (2 * i + par) * COLS) * YP + PAD) * C,
                                        [[C, P], [YP * C, COLS], [1, C]]), vrow[:, par]).then_inc(vrow_out[par], 16)
                for par in range(2):
                    sp.wait_ge(vrow_out[par], count((b + 1) * (8 * GROUPS)))

                def load_column(n, slot, earlier):
                    sp.wait_ge(v_in[slot % 2], count(16 * earlier))
                    sp.dma_start(vring[:, slot], at(vals, n * (YP * C), [[C, P], [1, TAPS * C]])) \
                      .then_inc(v_in[slot % 2], 16)

                def store_offsets(q, slot):
                    sp.wait_ge(off_ready, count(2 * (b * GROUPS + q) + 2))
                    sp.wait_ge(off_stored, count(16 * (b * GROUPS + q)))
                    sp.dma_start(off_out[slot].rearrange("(p k) t -> p (k t)", p=P),
                                 off[:, slot].rearrange("p r k t -> p (r k t)")).then_inc(off_stored, 16)

                store_offsets(0, 0)
                for n in range(AHEAD_V):
                    load_column(n, n, b * LOADS[n % 2] + n // 2)
                def columns(q, place, last=False):
                    for r in range(COLS):
                        n = COLS * q + r
                        sp.wait_ge(prod_ready, count(TAPS * (b * W + n)))
                        c = COLS * (place % 2) + r + AHEAD_V
                        load_column(n + AHEAD_V, c % RING, b * LOADS[c % 2] + (n + AHEAD_V) // 2
                                    if isinstance(q, int) else
                                    b * LOADS[c % 2] + COLS // 2 * q + (r + AHEAD_V) // 2)
                        if r == 1 and not last:
                            store_offsets(q + 1, (place + 1) % FAR_RING)

                with sp.Fori(0, GROUPS // FAR_RING - 1) as i:
                    for u in range(FAR_RING):
                        columns(FAR_RING * i + u, u)
                for q in range(GROUPS - FAR_RING, GROUPS):
                    columns(q, q % FAR_RING, last=q == GROUPS - 1)
                sp.wait_ge(res_ready, count((b + 1) * GROUPS))
                for n in range(4):
                    sp.dma_start(at(out, b * (C * PIX) + n * QUARTER, [[PIX, P], [1, QUARTER]]),
                                 x1[:, n * QUARTER:(n + 1) * QUARTER]).then_inc(stored, 16)
            sp.wait_ge(stored, count(64 * B))

        @block.gpsimd
        def _(pool):
            nc.gpsimd.memset(zeros, 0.0).then_inc(zeros_ready, 1)
            nc.gpsimd.memset(ones[:], 1.0).then_inc(ones_ready, 1)
            nc.gpsimd.memset(one_col[:, 0:1], 1.0).then_inc(ones_ready, 1)
            nc.gpsimd.memset(one_col[:, 1:2], -1.0).then_inc(ones_ready, 1)
            nc.gpsimd.memset(one_col[:, 2:3], 0.0).then_inc(ones_ready, 1)
            identity_matrix(nc, pool, ident, d_id)
            group_matrix(nc, pool, gmat, d_gm)
            n_const = 0
            one = [[1, 1]]
            for dst, pattern, base, mult in (
                    (keytab[:], [[1, KI]], 1, 0),
                    (row_at[:], one, 0, KI),
                    (first_at[:, :, 0], [[COLS, GROUPS]], 0, 0),
                    (first_at[:, :, 1], [[0, GROUPS]], 0, 1)):
                src = scratch[0:dst.shape[0], 0:dst.shape[1]]
                nc.gpsimd.iota(src, pattern=pattern, base=base, channel_multiplier=mult).then_inc(consts, 1)
                pool.wait_ge(consts, count(n_const + 1))
                nc.gpsimd.tensor_copy(dst, src).then_inc(consts, 1)
                pool.wait_ge(consts, count(n_const + 2))
                n_const += 2
            pool.wait_ge(w_in, count(16 * 8))
            pool.sem_inc(far_done, FAR_RING)
            with pool.Fori(0, B) as b:
                pool.wait_ge(x_in, count(64 * (b + 1)))
                pool.sem_inc(pool_passed, 1)
                with pool.Fori(0, NA) as i:
                    rows = x1[:, bass.ds(i * (COLS * W), COLS * W)].rearrange("p (r w) -> p r w", w=W)
                    nc.gpsimd.tensor_tensor(rows, rows, bproj_sb[:].unsqueeze(1).to_broadcast([P, COLS, W]),
                                            ALU.add).then_inc(b_added, 1)

                steps = [0]

                def step(ins):
                    steps[0] += 1
                    ins.then_inc(far_step, 1)

                def settle():
                    pool.wait_ge(far_step, steps[0])

                def then(ins):
                    step(ins)
                    settle()

                def restart():
                    steps[0] = 0
                    pool.sem_clear(far_step)
                    for s in (gathered, fetched):
                        pool.dma_reset(range(s.num, s.num + 1))
                        pool.sem_clear(s)

                def gather(dst, src, index, signal, offset=0):
                    pool.indirect_dma_start(out=dst, out_offset=None, in_=src,
                                            in_offset=bass.IndirectOffsetOnAxis(ap=index.bitcast(U32), axis=0),
                                            element_offset=offset).then_inc(signal, 16)

                table = vals.rearrange("x y (g c) -> (x y g) c", c=CG)

                def far_round(q, slot):
                    n = b * GROUPS + q
                    gather(i_sel[:], info_out, pos[:, 0:1], fetched)
                    gather(o_sel[:], off_out[slot], pos[:, 1:2], fetched)
                    pool.wait_ge(fetched, 32)
                    step(nc.gpsimd.tensor_tensor(wm[:], o_sel[:, 2:3], is_far[:], ALU.mult))
                    then(nc.gpsimd.tensor_tensor(loc[:], o_sel[:, 0:2], i_sel[:, 0:2], ALU.add))
                    then(nc.gpsimd.tensor_tensor(loc[:].unsqueeze(1), loc[:].unsqueeze(1),
                                                 first_at[:, bass.ds(q, 1), :], ALU.add))
                    then(nc.gpsimd.tensor_scalar(loc[:], loc[:], -1.0, float(W), ALU.max, ALU.min))
                    then(nc.gpsimd.tensor_copy(loci[:], loc[:]))
                    then(nc.gpsimd.tensor_copy(low[:], loci[:]))
                    then(nc.gpsimd.tensor_tensor(gap[:], low[:], loc[:], ALU.subtract))
                    then(nc.gpsimd.tensor_scalar(gap[:], gap[:], 0.0, None, ALU.is_gt))
                    then(nc.gpsimd.tensor_tensor(low[:], low[:], gap[:], ALU.subtract))
                    then(nc.gpsimd.tensor_scalar(idxf[:], low[:, 0:1], float(YP), low[:, 1:2], ALU.mult, ALU.add))
                    then(nc.gpsimd.tensor_scalar(idxf[:], idxf[:], float(G), i_sel[:, 2:3], ALU.mult, ALU.add))
                    then(nc.gpsimd.tensor_scalar(idx[:], idxf[:], float((PAD * YP + PAD) * G), None, ALU.add))
                    for dx in range(2):
                        for dy in range(2):
                            gather(gath[:, dx, dy, :], table, idx[:], gathered, (dx * YP + dy) * C)
                    then(nc.gpsimd.tensor_tensor(side[:, 1], loc[:], low[:], ALU.subtract))
                    then(nc.gpsimd.tensor_scalar(side[:, 0], side[:, 1], -1.0, 1.0, ALU.mult, ALU.add))
                    then(nc.gpsimd.tensor_scalar(wy[:], side[:, :, 1], wm[:, 0:1], None, ALU.mult))
                    then(nc.gpsimd.tensor_tensor(w4[:], side[:, :, 0].unsqueeze(2).to_broadcast([P, 2, 2]),
                                                 wy[:].unsqueeze(1).to_broadcast([P, 2, 2]), ALU.mult))
                    pool.wait_ge(gathered, 64)
                    then(nc.gpsimd.tensor_tensor(gath[:], gath[:], w4[:].unsqueeze(3).to_broadcast([P, 2, 2, CG]),
                                                 ALU.mult))
                    then(nc.gpsimd.tensor_tensor(gath[:, 0], gath[:, 0], gath[:, 1], ALU.add))
                    then(nc.gpsimd.tensor_tensor(gval[:], gath[:, 0, 0], gath[:, 0, 1], ALU.add))
                    then(nc.gpsimd.tensor_tensor(spread[:], i_sel[:, 4:].rearrange("p (r g) -> p r g", g=G)
                                                 .unsqueeze(3).to_broadcast([P, COLS, G, CG]),
                                                 gval[:].unsqueeze(1).unsqueeze(1)
                                                 .to_broadcast([P, COLS, G, CG]), ALU.mult))
                    pool.wait_ge(ssum_ready, count(n + 2))
                    pool.sem_inc(pool_passed, 1)
                    acc = ssum[:, slot].rearrange("p r (g c) -> p r g c", c=CG)
                    then(nc.gpsimd.tensor_tensor(acc, acc, spread[:], ALU.add))

                def far_rest(q, slot):
                    restart()
                    k = keys[:, slot]
                    then(nc.gpsimd.tensor_scalar(rest[:], k, least[:, slot:slot + 1], None, ALU.is_lt))
                    then(nc.gpsimd.tensor_tensor(k, k, rest[:], ALU.mult))
                    then(nc.gpsimd.tensor_reduce(key_sum[:], k, AX.C, ALU.add))
                    then(nc.gpsimd.tensor_copy(key_left[:], key_sum[:]))
                    with pool.Fori(0, KI) as j:
                        left = pool.value_load(key_left[0:1, bass.ds(j, 1)], min_val=0, max_val=P * KI)
                        with pool.If(left > 0):
                            restart()
                            then(nc.gpsimd.tensor_copy(is_far[:], keys[:, slot, bass.ds(j, 1)]))
                            then(nc.gpsimd.tensor_scalar(idxf[:], is_far[:], 1.0, 1.0, ALU.max, ALU.subtract))
                            step(nc.gpsimd.tensor_scalar(is_far[:], is_far[:], 0.5, None, ALU.is_gt))
                            step(nc.gpsimd.tensor_copy(pos[:, 0:1], idxf[:]))
                            then(nc.gpsimd.tensor_scalar(pos[:, 1:2], idxf[:], row_at[:, 0:1], None, ALU.add))
                            far_round(q, slot)

                with pool.Fori(0, GROUPS // FAR_RING) as i:
                    for slot in range(FAR_RING):
                        q = FAR_RING * i + slot
                        pool.wait_ge(cnt_ready, count(b * GROUPS + q + 1))
                        pool.sem_inc(pool_passed, 1)
                        n_rounds = pool.value_load(rounds[0:1, slot:slot + 1], min_val=0, max_val=8)
                        with pool.If(n_rounds > 0):
                            pool.wait_ge(off_stored, count(16 * (b * GROUPS + q + 1)))
                            pool.sem_inc(pool_passed, 1)
                            with pool.Fori(0, n_rounds) as t:
                                restart()
                                step(nc.gpsimd.tensor_copy(is_far[:], far[:, slot, bass.ds(t, 1)]))
                                then(nc.gpsimd.tensor_copy(pos[:].unsqueeze(2), far_at[:, slot, :, bass.ds(t, 1)]))
                                far_round(q, slot)
                            with pool.If(n_rounds > 7):
                                far_rest(q, slot)
                        pool.sem_inc(far_done, 1)

        @block.tensor
        def _(pe):
            pe.wait_ge(w_in, count(16 * 8))
            pe.wait_ge(d_id, count(2))
            pe.wait_ge(d_gm, count(3))
            pe.wait_ge(ones_ready, count(4))
            for ahead in (a_done, v_done, sum_done):
                pe.sem_inc(ahead, 1)
            with pe.Fori(0, B) as b:
                with pe.Fori(0, NA // 2) as i:
                    for par in range(2):
                        a = b * NA + 2 * i + par
                        pe.wait_ge(att_in[par], count(8 * (a - par) + 16))
                        pe.wait_ge(a_read, count(a))
                        for r in range(COLS):
                            mm = nc.tensor.matmul(sum_ps[:, par, r * W:(r + 1) * W], att[:, par, r, :], wproj_sb[:],
                                                  start=True, stop=True)
                        mm.then_inc(a_done, 1)
                pe.wait_ge(g_step, count(3 * b + 3))
                nc.tensor.matmul(a_ps[:, 0:2], gmat[:], ex[:], start=True, stop=True).then_inc(g_sum, 1)
                with pe.Fori(0, GROUPS // 2) as i:
                    for par in range(2):
                        v = b * GROUPS + 2 * i + par
                        pe.wait_ge(vn_ready, count(v + 1))
                        pe.wait_ge(vrow_ready, count(v))
                        for r in range(COLS):
                            mm = nc.tensor.matmul(sum_ps[:, par, r * C:(r + 1) * C], xn[:, par, r, :], wvalue_sb[:],
                                                  start=True, stop=True)
                        mm.then_inc(v_done, 1)

                def offsets(q, par):
                    n = b * GROUPS + q
                    pe.wait_ge(xn_ready, count(n + 1))
                    pe.wait_ge(off_ready, count(2 * n))
                    for r in range(COLS):
                        mm = nc.tensor.matmul(om_ps[:, r // 2, (r % 2) * OM:(r % 2 + 1) * OM], xn[:, par, r, :],
                                              wom_sb[:], start=True, stop=True)
                    mm.then_inc(om_done, 1)

                def count_far(q):
                    n = b * GROUPS + q
                    pe.wait_ge(flag_ready, count(n + 1))
                    pe.wait_ge(cnt_step, count(2 * n))
                    nc.tensor.matmul(cnt_ps[0:1, 0:8], ones[:], flag[:], start=True, stop=True) \
                      .then_inc(cnt_done, 1)

                def taps(q, par, r):
                    n = b * W + q * COLS + r
                    if r == 0:
                        pe.wait_ge(ssum_ready, count(b * GROUPS + q))
                    for dx in range(TAPS):
                        pe.wait_ge(prod_ready, count(TAPS * n + dx + 1))
                        for dy in range(TAPS):
                            mm = nc.tensor.matmul(sum_ps[:, par, r * C:(r + 1) * C], ident[:],
                                                  prod[:, r % 2, dx, dy * C:(dy + 1) * C],
                                                  start=(dx + dy == 0), stop=(dx + dy == 2 * TAPS - 2))
                    mm.then_inc(sum_done, 1)

                def turn(q, slot):
                    n = b * GROUPS + q
                    pe.wait_ge(far_done, count(n + 1 + FAR_RING))
                    pe.wait_ge(sT_ready, count(n))
                    for r in range(COLS):
                        mm = nc.tensor.transpose(t_ps[:, r * H:(r + 1) * H], ssum[:, slot, r, :], ident[:])
                    mm.then_inc(t_done, 1)

                def project(q):
                    n = b * GROUPS + q
                    pe.wait_ge(sT_ready, count(n + 1))
                    pe.wait_ge(res_ready, count(n))
                    nc.tensor.matmul(out_ps[:], wout_sb[:], sT[:], start=True, stop=True).then_inc(out_done, 1)

                def group(q, place, left=2, behind=LAG):
                    par = place % 2
                    for r in range(COLS):
                        if r == 3 and left >= 2:
                            offsets(q + 2, par)
                        taps(q, par, r)
                        if r == 0 and behind >= LAG:
                            turn(q - LAG, (place - LAG) % FAR_RING)
                        if r == 1 and left >= 1:
                            count_far(q + 1)
                        if r == 1 and behind >= LAG:
                            project(q - LAG)

                offsets(0, 0)
                count_far(0)
                offsets(1, 1)
                for q in range(LAG):
                    group(q, q, behind=q)
                with pe.Fori(0, LOOPS) as i:
                    for u in range(LAG, LAG + FAR_RING):
                        group(FAR_RING * i + u, u % FAR_RING)
                for q in range(LAG + LOOPS * FAR_RING, GROUPS):
                    group(q, q % FAR_RING, left=GROUPS - 1 - q)
                for q in range(GROUPS - LAG, GROUPS):
                    turn(q, q % FAR_RING)
                    project(q)

        @block.scalar
        def _(act):
            act.wait_ge(ones_ready, count(4))
            act.sem_inc(ssum_ready, 1)
            with act.Fori(0, B) as b:
                act.wait_ge(g_sq, count(2 * b + 1))
                nc.scalar.activation(gv[:, 1:2], gv[:, 0:1], ACT.Sqrt).then_inc(g_root, 1)
                act.wait_ge(g_sq, count(2 * b + 2))
                with act.Fori(0, GROUPS // 2) as i:
                    for par in range(2):
                        v = b * GROUPS + 2 * i + par
                        act.wait_ge(v_done, count(v))
                        nc.scalar.activation(xn[:, par], cols[:, bass.ds((2 * i + par) * COLS, COLS), :],
                                             ACT.Identity, bias=gn[:, 1:2], scale=gn[:, 0:1]).then_inc(vn_ready, 1)
                act.wait_ge(v_done, count((b + 1) * GROUPS + 1))

                def normalise(q, par, older):
                    act.wait_ge(om_done, count(older))
                    src = cols[:, q * COLS:(q + 1) * COLS, :] if isinstance(q, int) else \
                        cols[:, bass.ds(q * COLS, COLS), :]
                    nc.scalar.activation(xn[:, par], src, ACT.Identity, bias=gn[:, 1:2],
                                         scale=gn[:, 0:1]).then_inc(xn_ready, 1)

                def xy(t):
                    return t.rearrange("p r (t k) -> p r t k", t=2)

                def hats(q, place):
                    n = b * GROUPS + q
                    act.wait_ge(off_ready, count(2 * n + 2))
                    act.wait_ge(near_step, count(3 * n))
                    o = off[:, place].rearrange("p r k t -> p r t k")[:, :, 0:2, :]
                    nc.scalar.activation(xy(dist[:, 0]), o, ACT.Abs, bias=one_col[:, 0:1]).then_inc(dist_ready, 1)
                    nc.scalar.activation(xy(dist[:, 1]), o, ACT.Abs).then_inc(dist_ready, 1)
                    nc.scalar.activation(xy(dist[:, 2]), o, ACT.Abs, bias=one_col[:, 1:2]).then_inc(dist_ready, 1)
                    act.wait_ge(wt_ready, count(n))
                    for j in range(3):
                        act.wait_ge(dist_ready, count(3 * n + 1 + j))
                        nc.scalar.activation(hat[:, j], dist[:, j], ACT.Relu, bias=one_col[:, 0:1],
                                             scale=-1.0).then_inc(hat_ready, 1)

                def clear_weights(q, par):
                    nc.scalar.copy(wt[:, par].rearrange("p r a k -> p (r a k)"),
                                   one_col[:, 2:3].to_broadcast([P, COLS * TAPS * TAPS * G])).then_inc(wt_zero, 1)

                def read_sums(q, place):
                    act.wait_ge(sum_done, count((b * GROUPS + q + 1) * COLS + 1))
                    nc.scalar.copy(ssum[:, place], sum_ps[:, place % 2].rearrange("p (r c) -> p r c", c=C)) \
                      .then_inc(ssum_ready, 1)

                def read_turned(q):
                    n = b * GROUPS + q
                    act.wait_ge(t_done, count(n + 1))
                    act.wait_ge(out_done, count(n))
                    nc.scalar.copy(sT[:], t_ps[:]).then_inc(sT_ready, 1)

                def group(q, place, left=2, behind=LAG):
                    if behind >= 1:
                        read_sums(q - 1, (place - 1) % FAR_RING)
                    if left >= 1:
                        clear_weights(q + 1, (place + 1) % 2)
                    if left >= 2:
                        normalise(q + 2, place % 2, b * GROUPS + q + 1)
                    if left >= 1:
                        hats(q + 1, (place + 1) % FAR_RING)
                    if behind >= LAG:
                        read_turned(q - LAG)

                normalise(0, 0, b * GROUPS)
                normalise(1, 1, b * GROUPS)
                clear_weights(0, 0)
                hats(0, 0)
                for q in range(LAG):
                    group(q, q, behind=q)
                with act.Fori(0, LOOPS) as i:
                    for u in range(LAG, LAG + FAR_RING):
                        group(FAR_RING * i + u, u % FAR_RING)
                for q in range(LAG + LOOPS * FAR_RING, GROUPS):
                    group(q, q % FAR_RING, left=GROUPS - 1 - q)
                read_sums(GROUPS - 1, (GROUPS - 1) % FAR_RING)
                for q in range(GROUPS - LAG, GROUPS):
                    read_turned(q)

        @block.vector
        def _(dve):
            dve.wait_ge(w_in, count(16 * 8))
            for ahead in (a_read, vrow_ready):
                dve.sem_inc(ahead, 1)
            NORM, STEPS = 9, 12
            with dve.Fori(0, B) as b:
                with dve.Fori(0, NA // 2) as i:
                    for par in range(2):
                        ai = 2 * i + par
                        a = b * NA + ai
                        dve.wait_ge(a_done, count(a + 2))
                        dve.wait_ge(b_added, count(a + 1))
                        rows = x1[:, bass.ds(ai * (COLS * W), COLS * W)]
                        nc.vector.tensor_tensor(rows, sum_ps[:, par], rows, ALU.add).then_inc(a_read, 1)
                        dve.wait_ge(a_read, count(a + 2))
                        nc.vector.bn_stats(bn[:, bass.ds(ai, 1), :].rearrange("p a b -> p (a b)"), rows) \
                          .then_inc(x1_ready, 1)
                dve.wait_ge(x1_ready, count(NA * (b + 1)))
                dve.sem_inc(dve_passed, 1)
                nc.vector.bn_aggr(mv[:], bn[:].rearrange("p a b -> p (a b)")).then_inc(g_step, 1)
                dve.wait_ge(g_step, count(3 * b + 1))
                nc.vector.tensor_copy(ex[:, 0:1], mv[:, 0:1]).then_inc(g_step, 1)
                nc.vector.scalar_tensor_tensor(out=ex[:, 1:2], in0=mv[:, 0:1], scalar=mv[:, 0:1], in1=mv[:, 1:2],
                                               op0=ALU.mult, op1=ALU.add).then_inc(g_step, 1)
                dve.wait_ge(g_sum, count(b + 1))
                group_scales(nc, dve, a_ps[:, 0:2], gst, gv, gn[:, 0:1], gn[:, 1:2], coef_step, b * (NORM + STEPS * GROUPS),
                             g_sq, 2 * b, g_root, b)

                with dve.Fori(0, GROUPS // 2) as i:
                    for par in range(2):
                        v = b * GROUPS + 2 * i + par
                        dve.wait_ge(v_done, count(v + 2))
                        dve.wait_ge(vrow_out[par], count(b * (8 * GROUPS) + 16 * i))
                        nc.vector.tensor_tensor(vrow[:, par], sum_ps[:, par].rearrange("p (r c) -> p r c", c=C),
                                                bvalue_sb[:].unsqueeze(1).to_broadcast([P, COLS, C]),
                                                ALU.add).then_inc(vrow_ready, 1)

                def read_offsets(q, place):
                    n = b * GROUPS + q
                    dve.wait_ge(om_done, count(n + 1))
                    dve.wait_ge(far_done, count(n + 1))
                    for half in range(2):
                        nc.vector.tensor_tensor(off[:, place, 2 * half:2 * half + 2],
                                                om_ps[:, half, 0:2 * OM].rearrange("p (r k t) -> p r k t", k=KG, t=3),
                                                bom_sb[:].rearrange("p (k t) -> p k t", t=3).unsqueeze(1)
                                                .to_broadcast([P, 2, KG, 3]),
                                                ALU.add).then_inc(off_ready, 1)

                def masks(q, place):
                    n = b * GROUPS + q
                    dve.wait_ge(dist_ready, count(3 * n + 2))
                    nc.vector.tensor_tensor(reach[:], dist[:, 1, :, 0:KG], dist[:, 1, :, KG:], ALU.max) \
                      .then_inc(near_step, 1)
                    dve.wait_ge(near_step, count(3 * n + 1))
                    nc.vector.scalar_tensor_tensor(out=keys[:, place].rearrange("p (r k) -> p r k", k=KG),
                                                   in0=reach[:], scalar=1.0,
                                                   in1=keytab[:].rearrange("p (r k) -> p r k", k=KG),
                                                   op0=ALU.is_gt, op1=ALU.mult).then_inc(near_step, 1)
                    nc.vector.scalar_tensor_tensor(out=mf[:, place % 2], in0=reach[:], scalar=1.0,
                                                   in1=off[:, place, :, :, 2],
                                                   op0=ALU.is_le, op1=ALU.mult).then_inc(near_step, 1)
                    dve.wait_ge(near_step, count(3 * n + 3))
                    dve.sem_inc(dve_passed, 1)
                    nc.vector.max(top[:], keys[:, place]).then_inc(top_ready, 1)

                def flags(q, place):
                    n = b * GROUPS + q
                    dve.wait_ge(top_ready, count(n + 1))
                    dve.wait_ge(cnt_done, count(n))
                    nc.vector.tensor_scalar(flag[:], top[:], 0.5, None, ALU.is_gt).then_inc(flag_ready, 1)
                    nc.vector.tensor_scalar(far[:, place], top[:], 0.5, None, ALU.is_gt).then_inc(key_ready, 1)
                    nc.vector.tensor_copy(least[:, place:place + 1], top[:, 7:8]).then_inc(key_ready, 1)
                    nc.vector.tensor_scalar(at8[:], top[:], 1.0, 1.0, ALU.max, ALU.subtract).then_inc(key_ready, 1)
                    dve.wait_ge(key_ready, count(5 * n + 3))
                    nc.vector.tensor_copy(far_at[:, place, 0], at8[:]).then_inc(key_ready, 1)
                    nc.vector.tensor_scalar(far_at[:, place, 1], at8[:], row_at[:, 0:1], None, ALU.add) \
                      .then_inc(key_ready, 1)

                def read_counts(q, place):
                    n = b * GROUPS + q
                    dve.wait_ge(cnt_done, count(n + 1))
                    nc.vector.tensor_scalar(some[:], cnt_ps[0:1, 0:8], 0.5, None, ALU.is_gt).then_inc(cnt_step, 1)
                    dve.wait_ge(cnt_step, count(2 * n + 1))
                    nc.vector.tensor_reduce(total[:], some[:], AX.X, ALU.add).then_inc(cnt_step, 1)
                    dve.wait_ge(cnt_step, count(2 * n + 2))
                    dve.wait_ge(key_ready, count(5 * n + 5))
                    nc.vector.tensor_copy(rounds[:, place:place + 1], total[:]).then_inc(cnt_ready, 1)

                def tap_terms(q, par):
                    n = b * GROUPS + q
                    s = b * (NORM + STEPS * GROUPS) + NORM + STEPS * q
                    dve.wait_ge(hat_ready, count(3 * n + 3))
                    nc.vector.tensor_tensor(my[:], hat[:, :, :, KG:], mf[:, par].unsqueeze(1)
                                            .to_broadcast([P, 3, COLS, KG]), ALU.mult).then_inc(coef_step, 1)
                    dve.wait_ge(coef_step, count(s + 1))
                    for jx in range(3):
                        nc.vector.tensor_tensor(tt[:, jx], hat[:, jx, :, 0:KG].unsqueeze(1)
                                                .to_broadcast([P, 3, COLS, KG]), my[:], ALU.mult) \
                          .then_inc(coef_step, 1)

                def weight_term(q, par, i):
                    s = b * (NORM + STEPS * GROUPS) + NORM + STEPS * q
                    jx, jy = divmod(i, 3)
                    if i == 0:
                        dve.wait_ge(wt_zero, count(b * GROUPS + q + 1))
                    dve.wait_ge(coef_step, count(s + 4 + i))
                    acc = wt[:, par, :, jx:jx + KS, jy * G:(jy + KS) * G]
                    nc.vector.tensor_tensor(acc, acc, tt[:, jx, jy].rearrange("p r (a k) -> p r a k", a=KS),
                                            ALU.add).then_inc(coef_step if i < 8 else wt_ready, 1)

                def products(q, par, r, terms=()):
                    slot = (COLS * par + r) % RING
                    if r == 0:
                        dve.wait_ge(wt_ready, count(b * GROUPS + q + 1))
                    dve.wait_ge(v_in[(r + 1) % 2], count(16 * (b * LOADS[(r + 1) % 2] + 2 * q + (r + 3) // 2 + 1)))
                    dve.wait_ge(v_in[r % 2], count(16 * (b * LOADS[r % 2] + 2 * q + r // 2 + 3)))
                    dve.wait_ge(sum_done, count(b * W + q * COLS + r))
                    for dx in range(TAPS):
                        nc.vector.tensor_tensor(
                            prod[:, r % 2, dx].rearrange("p (t c) -> p t c", c=CG),
                            vring[:, (slot + dx) % RING].rearrange("p (t c) -> p t c", c=CG),
                            wt[:, par, r, dx].unsqueeze(2).to_broadcast([P, TAPS * G, CG]), ALU.mult) \
                          .then_inc(prod_ready, 1)
                        if dx < len(terms):
                            weight_term(q + 1, 1 - par, terms[dx])

                def result(q):
                    n = b * GROUPS + q
                    dve.wait_ge(out_done, count(n + 1))
                    dst = cols[:, q * COLS:(q + 1) * COLS, :] if isinstance(q, int) else \
                        cols[:, bass.ds(q * COLS, COLS), :]
                    nc.vector.scalar_tensor_tensor(out=dst, in0=out_ps[:].rearrange("p (r y) -> p r y", y=H),
                                                   scalar=bout_sb[:, 0:1], in1=dst, op0=ALU.add,
                                                   op1=ALU.add).then_inc(res_ready, 1)

                def group(q, place, first=False, last=False):
                    par, after = place % 2, (place + 1) % FAR_RING
                    products(q, par, 0)
                    read_counts(q, place)
                    if not last:
                        read_offsets(q + 1, after)
                    products(q, par, 1)
                    if not last:
                        masks(q + 1, after)
                        flags(q + 1, after)
                        tap_terms(q + 1, 1 - par)
                    products(q, par, 2, () if last else range(TAPS))
                    products(q, par, 3, () if last else range(TAPS, 9))
                    if not first:
                        result(q - LAG)

                read_offsets(0, 0)
                masks(0, 0)
                flags(0, 0)
                tap_terms(0, 0)
                for i in range(9):
                    weight_term(0, 0, i)
                for q in range(LAG):
                    group(q, q, first=True)
                with dve.Fori(0, (GROUPS - LAG - 1) // FAR_RING) as i:
                    for u in range(LAG, LAG + FAR_RING):
                        group(FAR_RING * i + u, u % FAR_RING)
                group(GROUPS - 1, (GROUPS - 1) % FAR_RING, last=True)
                for q in range(GROUPS - LAG, GROUPS):
                    result(q)


def program(nc, x, w_qkv, b_qkv, bv, rel, w_proj, b_proj, w_value, b_value, w_om, b_om, w_out, b_out, out):
    attended = nc.dram_tensor("attended", (B, H, W, C), F32, kind="Internal").ap()
    rel_rows = nc.dram_tensor("rel_rows", (WS, NH * REL * WS), F32, kind="Internal").ap()
    parts_dram = nc.dram_tensor("parts_dram", (2, P, 3 * 2 * 2 * NT), BF16, kind="Internal").ap()
    vals = nc.dram_tensor("vals", (XP, YP, C), F32, kind="Internal").ap()
    off_out = [nc.dram_tensor(f"off_out{n}", (P * COLS * KG, 3), F32, kind="Internal").ap()
               for n in range(FAR_RING)]
    info_out = nc.dram_tensor("info_out", (COLS * KG, 4 + COLS * G), F32, kind="Internal").ap()
    attention(nc, x, w_qkv, b_qkv, bv, rel, attended, rel_rows, parts_dram, info_out)
    deformable(nc, x, attended, w_proj, b_proj, w_value, b_value, w_om, b_om, w_out, b_out, vals,
               off_out, info_out, out)


_OUT = ((B, C, H, W), "float32")


def kernel(x, L0_conv_qkv_w, L0_conv_qkv_b, L0_conv_proj_w, L0_conv_proj_b, L0_conv_bias_table,
           L1_conv_value_proj_w, L1_conv_value_proj_b, L1_conv_offset_mask_w, L1_conv_offset_mask_b,
           L1_conv_output_proj_w, L1_conv_output_proj_b):
    import numpy as np
    import concourse.bacc as bacc
    from concourse.bass_utils import run_bass_kernel_spmd

    def layout(a, *order):
        return np.ascontiguousarray(np.transpose(np.asarray(a), order) if order else np.asarray(a))

    g, ky, kx = np.meshgrid(np.arange(G), np.arange(KS), np.arange(KS), indexing="ij")
    point = ky * KS + kx
    rows = [g * 3 * K2 + 2 * point, g * 3 * K2 + 2 * point + 1, g * 3 * K2 + 2 * K2 + point]
    order = np.stack([np.transpose(r, (2, 1, 0)) for r in rows], axis=-1).reshape(-1)
    arrays = {
        "x": layout(x),
        "w_qkv": layout(L0_conv_qkv_w, 1, 0),
        "b_qkv": layout(np.asarray(L0_conv_qkv_b).reshape(3, C), 1, 0),
        "bv": layout(np.asarray(L0_conv_qkv_b)[2 * C:]),
        "rel": layout(np.asarray(L0_conv_bias_table).reshape(REL, REL, NH)[::-1, ::-1], 2, 0, 1).reshape(-1),
        "w_proj": layout(L0_conv_proj_w, 1, 0),
        "b_proj": layout(L0_conv_proj_b),
        "w_value": layout(L1_conv_value_proj_w, 1, 0),
        "b_value": layout(L1_conv_value_proj_b),
        "w_om": layout(np.asarray(L1_conv_offset_mask_w)[order], 1, 0),
        "b_om": layout(np.asarray(L1_conv_offset_mask_b)[order]),
        "w_out": layout(L1_conv_output_proj_w, 1, 0),
        "b_out": layout(np.asarray(L1_conv_output_proj_b).reshape(C, 1)),
    }
    nc = bacc.Bacc("TRN2", target_bir_lowering=False, num_devices=1)
    ins = {n: nc.dram_tensor(n, a.shape, F32, kind="ExternalInput").ap() for n, a in arrays.items()}
    out = nc.dram_tensor("out", _OUT[0], F32, kind="ExternalOutput").ap()
    program(nc, out=out, **ins)
    result = run_bass_kernel_spmd(nc, [arrays], core_ids=[0])
    return result.results[0]["out"]
```
